# Optimizing a Trainium2 kernel written in Bass

```python
import numpy as np
import jax
import jax.numpy as jnp

def _softmax(x, axis=-1):
    return jax.nn.softmax(x, axis=axis)

def _gelu(x):
    return jax.nn.gelu(x, approximate=True)

def _silu(x):
    return jax.nn.silu(x)

def _sigmoid(x):
    return jax.nn.sigmoid(x)

def _layernorm(x, axis=-1, eps=1e-05):
    m = jnp.mean(x, axis=axis, keepdims=True)
    v = jnp.var(x, axis=axis, keepdims=True)
    return (x - m) / jnp.sqrt(v + eps)

def _scatter_add(tgt, idx, src, axis=0):
    return tgt.at[idx].add(src)

def _segment_sum(src, seg, n):
    return jax.ops.segment_sum(src, seg, n)
kernel_name = 'mk_adj_preln_d2_adj_r2_a641c5'

def setup_inputs(seed: int=0):
    np.random.seed(seed)
    _w = jnp.asarray

    def _rec_inputs():
        import jax
        import jax.numpy as jnp
        _gk = jax.random.key(seed)
        x = -0.0001538 + 1 * jax.random.normal(jax.random.fold_in(_gk, 1), (16, 512, 384), jnp.float32)
        _a = jax.random.bernoulli(jax.random.fold_in(_gk, 2), 0.0078125, (16, 512, 512))
        _a = jnp.logical_or(_a, jnp.swapaxes(_a, -1, -2))
        _a = jnp.logical_or(_a, jnp.eye(512, dtype=bool))
        _af = _a.astype(jnp.float32)
        _af = _af * jax.random.uniform(jax.random.fold_in(_gk, 3), (16, 512, 512), jnp.float32, 0.05, 0.999992)
        adj = _af
        return (x, adj)
    x, adj = _rec_inputs()

    def _L0_gnn_setup():
        import jax, jax.numpy as jnp
        import numpy as np
        B, N, D, H = (8, 512, 384, 12)
        HD = D // H

        def _split_heads(x):
            b, n, _ = x.shape
            return x.reshape(b, n, H, HD).transpose(0, 2, 1, 3)
        key = jax.random.key(seed)
        ks = jax.random.split(key, 10)
        input_graph = jax.random.normal(ks[0], (B, N, D), dtype=jnp.float32)
        u = jax.random.uniform(ks[1], (B, N, N), dtype=jnp.float32)
        keep = jax.random.uniform(ks[2], (B, N, N)) < 0.15
        adj = jnp.where(keep, u, 0.0)
        s = 1.0 / np.sqrt(D)
        Wq = jax.random.normal(ks[3], (D, D), dtype=jnp.float32) * s
        bq = jnp.zeros((D,), dtype=jnp.float32)
        Wk = jax.random.normal(ks[4], (D, D), dtype=jnp.float32) * s
        bk = jnp.zeros((D,), dtype=jnp.float32)
        Wv = jax.random.normal(ks[5], (D, D), dtype=jnp.float32) * s
        bv = jnp.zeros((D,), dtype=jnp.float32)
        beta = jnp.asarray(0.1, dtype=jnp.float32)
        return {'input_graph': input_graph, 'adj': adj, 'Wq': Wq, 'bq': bq, 'Wk': Wk, 'bk': bk, 'Wv': Wv, 'bv': bv, 'beta': beta}
    _L0_gnn_all = _L0_gnn_setup()
    _L0_gnn_in = {k: v for k, v in _L0_gnn_all.items() if k in ('Wq', 'bq', 'Wk', 'bk', 'Wv', 'bv', 'beta')}
    del _L0_gnn_all

    def _L1_gnn_setup():
        import jax, jax.numpy as jnp
        import numpy as np
        NUM_HEADS = 12
        HIDDEN = 384
        HEAD = HIDDEN // NUM_HEADS
        B, N = (16, 256)
        key = jax.random.key(seed)
        ks = jax.random.split(key, 9)
        s = 0.02
        return {'x': jax.random.normal(ks[0], (B, N, HIDDEN), jnp.float32), 'spatial_encoding': jax.random.normal(ks[1], (B, N, N), jnp.float32), 'edge_encoding': jax.random.normal(ks[2], (B, N, N), jnp.float32), 'Wq': jax.random.normal(ks[3], (HIDDEN, HIDDEN), jnp.float32) * s, 'Wk': jax.random.normal(ks[4], (HIDDEN, HIDDEN), jnp.float32) * s, 'Wv': jax.random.normal(ks[5], (HIDDEN, HIDDEN), jnp.float32) * s, 'bv': jax.random.normal(ks[6], (HIDDEN,), jnp.float32) * s, 'Wo': jax.random.normal(ks[7], (HIDDEN, HIDDEN), jnp.float32) * s, 'bo': jax.random.normal(ks[8], (HIDDEN,), jnp.float32) * s}
    _L1_gnn_all = _L1_gnn_setup()
    _L1_gnn_in = {k: v for k, v in _L1_gnn_all.items() if k in ('Wq', 'Wk', 'Wv', 'bv', 'Wo', 'bo')}
    del _L1_gnn_all
    return {'x': x, 'adj': adj, 'L0_gnn_Wq': _L0_gnn_in['Wq'], 'L0_gnn_bq': _L0_gnn_in['bq'], 'L0_gnn_Wk': _L0_gnn_in['Wk'], 'L0_gnn_bk': _L0_gnn_in['bk'], 'L0_gnn_Wv': _L0_gnn_in['Wv'], 'L0_gnn_bv': _L0_gnn_in['bv'], 'L0_gnn_beta': _L0_gnn_in['beta'], 'L1_gnn_Wq': _L1_gnn_in['Wq'], 'L1_gnn_Wk': _L1_gnn_in['Wk'], 'L1_gnn_Wv': _L1_gnn_in['Wv'], 'L1_gnn_bv': _L1_gnn_in['bv'], 'L1_gnn_Wo': _L1_gnn_in['Wo'], 'L1_gnn_bo': _L1_gnn_in['bo']}

def reference(x, adj, L0_gnn_Wq, L0_gnn_bq, L0_gnn_Wk, L0_gnn_bk, L0_gnn_Wv, L0_gnn_bv, L0_gnn_beta, L1_gnn_Wq, L1_gnn_Wk, L1_gnn_Wv, L1_gnn_bv, L1_gnn_Wo, L1_gnn_bo):
    import jax
    import jax.numpy as jnp

    def _L0_gnn_ref(input_graph, adj, Wq, bq, Wk, bk, Wv, bv, beta):
        import jax, jax.numpy as jnp
        import numpy as np
        B, N, D, H = (8, 512, 384, 12)
        HD = D // H

        def _split_heads(x):
            b, n, _ = x.shape
            return x.reshape(b, n, H, HD).transpose(0, 2, 1, 3)
        q = _split_heads(input_graph @ Wq + bq)
        k = _split_heads(input_graph @ Wk + bk)
        v = _split_heads(input_graph @ Wv + bv)
        scores = jnp.einsum('bhqd,bhkd->bhqk', q, k) / jnp.sqrt(jnp.asarray(HD, input_graph.dtype))
        adj_e = adj[:, None, :, :]
        scores = scores + beta * adj_e
        scores = jnp.where(adj_e > 0, scores, jnp.asarray(-9000000000000000.0, scores.dtype))
        probs = jax.nn.softmax(scores, axis=-1)
        out = jnp.einsum('bhqk,bhkd->bhqd', probs, v)
        return out.transpose(0, 2, 1, 3).reshape(input_graph.shape[0], input_graph.shape[1], D)

    def _L1_gnn_ref(x, spatial_encoding, edge_encoding, Wq, Wk, Wv, bv, Wo, bo):
        import jax, jax.numpy as jnp
        import numpy as np
        NUM_HEADS = 12
        HIDDEN = 384
        HEAD = HIDDEN // NUM_HEADS
        B, N = (16, 256)
        b, n, h = x.shape
        scale = jnp.asarray(HIDDEN, x.dtype) ** (-0.5)
        q = (x @ Wq.T).reshape(b, n, NUM_HEADS, HEAD)
        k = (x @ Wk.T).reshape(b, n, NUM_HEADS, HEAD)
        v = (x @ Wv.T + bv).reshape(b, n, NUM_HEADS, HEAD)
        bias = (spatial_encoding + edge_encoding)[:, None]
        scores = jnp.einsum('bqhd,bkhd->bhqk', q, k) * scale + bias
        row_nonzero = jnp.any(scores != 0, axis=-1, keepdims=True)
        scores = jnp.where(row_nonzero, scores, -jnp.inf)
        p = jax.nn.softmax(scores, axis=-1)
        p = jnp.nan_to_num(p)
        out = jnp.einsum('bhqk,bkhd->bqhd', p, v).reshape(b, n, h)
        return out @ Wo.T + bo
    h = jnp.maximum(_layernorm(x, axis=-1), 0.0)
    x = x + _L0_gnn_ref(h, adj, L0_gnn_Wq, L0_gnn_bq, L0_gnn_Wk, L0_gnn_bk, L0_gnn_Wv, L0_gnn_bv, L0_gnn_beta)
    h = jnp.maximum(_layernorm(x, axis=-1), 0.0)
    x = x + _L1_gnn_ref(h, adj, adj, L1_gnn_Wq, L1_gnn_Wk, L1_gnn_Wv, L1_gnn_bv, L1_gnn_Wo, L1_gnn_bo)
    return x

_drawn_inputs = setup_inputs


def setup_inputs(seed=0):
    import zlib

    import numpy as np

    out = dict(_drawn_inputs(seed))
    spreads = {'L0_gnn_bq': (0.0, 0.75), 'L0_gnn_bk': (0.0, 2.0), 'L0_gnn_bv': (0.0, 0.1)}
    factors = {'L1_gnn_Wq': 61.59, 'L1_gnn_Wk': 61.905, 'L1_gnn_bv': 6.904, 'L1_gnn_bo': 3.283}
    for name, (base, spread) in spreads.items():
        noise = np.random.default_rng([zlib.crc32(name.encode()), seed]).standard_normal(out[name].shape)
        drawn = base * np.exp(spread * noise) if base else spread * noise
        out[name] = jnp.asarray(drawn.astype(out[name].dtype))
    for name, factor in factors.items():
        out[name] = (out[name] * factor).astype(out[name].dtype)
    return out
```

```python
from contextlib import ExitStack

import concourse.bass as bass
from concourse import mybir
import numpy as np

F32 = mybir.dt.float32
F32R = mybir.dt.float32r
ALU = mybir.AluOpType
ACT = mybir.ActivationFunctionType
AX = mybir.AxisListType

B, N, D, H = 16, 512, 384, 12
HD = D // H
P = 128
T = N // P
C = D // P
GH = P // HD
G = H // GH
STEPS = H * T
PAIRS = H // 2
EPS = 1e-5
MASKED = -9000000000000000.0
BIG = 3.0e38
SPLIT_ROWS = 3 * HD
STACKS = 6

LAG_TURN = 2
LAG_LO = 3
LAG_WEIGH = 6
LAG_COPY, LAG_OUT, LAG_NORM = T + 6, T + 7, T + 8
TAIL = LAG_NORM + 1


class Graph:

    def __init__(self, c, i=None):
        self.c, self.i = c, i

    def next(self):
        return Graph(self.c + 1, self.i)

    def prev(self):
        return Graph(self.c - 1, self.i)

    def exists(self):
        return self.i is not None or 0 <= self.c < B

    def slot(self):
        return self.c % 2

    def number(self):
        return self.c if self.i is None else self.i * 2 + self.c

    def count(self, per_graph, more):
        c = self.c * per_graph + more
        assert self.i is None or c > 0, "a wait on zero"
        return c if self.i is None else self.i * (2 * per_graph) + c

    def slot_count(self, by):
        c = by * (self.c // 2 + 1)
        return c if self.i is None else self.i * by + c

    def group_slot(self, g):
        return (G * self.c + g) % 2

    def group_count(self, g, by, back=0):
        c = by * ((G * self.c + g - back) // 2 + 1)
        return c if self.i is None else self.i * (G * by) + c


def wait(eng, sem, value):
    if not isinstance(value, int) or value > 0:
        eng.wait_ge(sem, value)


def side_steps(layer):
    if layer == 0:
        tasks = [(2 + t, "value", t, 0) for t in range(T)]
        tasks += [(8, "qk", 2, 0), (10, "qk", 3, 0), (18, "qk", 4, 0), (20, "qk", 5, 0)]
        tasks += [(24 + 2 * t, "turn_h", t, 1) for t in range(T)]
        tasks += [(36, "qk", 0, 1), (38, "qk", 1, 1)]
        return tasks, 20
    tasks = [(2 + t, "value", t, 0) for t in range(T)]
    tasks += [(6, "qk", 2, 0), (7, "qk", 3, 0)]
    tasks += [(9, "turn_a", 0, -1), (10, "turn_a", 1, -1), (11, "project", 0, -1), (12, "turn_a", 2, -1),
              (13, "project", 1, -1), (14, "turn_a", 3, -1), (15, "project", 2, -1), (17, "project", 3, -1)]
    tasks += [(20, "qk", 4, 0), (22, "qk", 5, 0)]
    tasks += [(30 + 2 * t, "turn_h", t, 1) for t in range(T)]
    tasks += [(39, "qk", 0, 1), (41, "qk", 1, 1)]
    return tasks, 26


def layer_pass(nc, layer, x_in, adj, w_in, b_in, beta, x_out):
    first = layer == 0
    side, stats_step = side_steps(layer)
    assert len(side) % 2 == 0
    names = ["q", "k", "v"] + ([] if first else ["o"])
    scale = {n: 1.0 for n in names}
    scale["q"] = float(np.float32(HD ** -0.5)) if first else float(np.float32(D ** -0.5)) / 2
    negate = -1.0 if first else -2.0

    ctx = ExitStack()
    with ctx:
        def sb(name, shape, dt=F32):
            return ctx.enter_context(nc.sbuf_tensor(f"{name}_{layer}", shape, dt))

        def psum(name, shape):
            return ctx.enter_context(nc.psum_tensor(f"{name}_{layer}", shape, F32))

        def sem(name):
            return ctx.enter_context(nc.semaphore(f"{name}_{layer}"))

        x_sb = sb("x", [P, 2, T, D])
        bias = sb("bias", [P, 2, T, N])
        w_raw = sb("w_raw", [P, C, D])
        w_hi = {n: sb(f"w{n}_hi", [P, C, D], F32R) for n in names}
        w_lo = {n: sb(f"w{n}_lo", [P, C, D], F32R) for n in names}
        h = sb("h", [P, 2, D])
        ht_hi, ht_lo = (sb(f"ht_{s}", [P, C, N], F32R) for s in ("hi", "lo"))
        qk_hi, qk_lo = (sb(f"qk_{s}", [P, 2, N], F32R) for s in ("hi", "lo"))
        q_stack, k_stack = (sb(f"{s}_stack", [SPLIT_ROWS, 2, GH, N], F32R) for s in "qk")
        v_stack = sb("v_stack", [P, T, PAIRS, 3, 2 * HD], F32R)
        masked = sb("masked", [P, 4, N])
        probs = sb("probs", [P, 4, N])
        pt_hi, pt_lo = (sb(f"pt_{s}", [P, 2, T, N], F32R) for s in ("hi", "lo"))
        out_t = sb("out_t", [P, N])
        neg_max = sb("neg_max", [P, 2, H, T])
        sums = sb("sums", [P, 2, H, T])
        rsum = sb("rsum", [P, 2, 2, T])
        stat = sb("stat", [P, T, 6])
        mean_var = sb("mean_var", [P, T, 2])
        var_eps, root0, sq, half_var, prod, fix, rstd, neg_mean, shift = (
            sb(n, [P, T]) for n in ("var_eps", "root0", "sq", "half_var", "prod", "fix", "rstd", "neg_mean", "shift"))
        eps, neg_half, one_half = (sb(n, [P, T]) for n in ("eps", "neg_half", "one_half"))
        ident = sb("ident", [P, P])
        fold = sb("fold", [P, 2 * HD])
        one_rows = sb("one_rows", [P, P], F32R)
        row_raw = sb("row_raw", [1, D])
        v_row = sb("v_row", [P, D], F32R)
        if first:
            qk_bias = sb("qk_bias", [P, 2, G])
            beta_col = sb("beta_col", [P, 1])
            scaled, hole = sb("scaled", [P, N]), sb("hole", [P, N])
            update = sb("update", [P, 2, T, 2 * HD])
        else:
            o_row = sb("o_row", [P, D], F32R)
            attn = sb("attn", [P, T, D])
            at_hi, at_lo = (sb(f"at_{s}", [P, 2, C, P], F32R) for s in ("hi", "lo"))
            halves = sb("halves", [P, 2, T, N // 2])
            total = sb("total", [P, 2, H, T])
            size = sb("size", [P, 2, T])
            kept = sb("kept", [P, 2, 2, T])

        s_ps, t_ps, m_ps = (psum(n, [P, 2, N]) for n in ("s_ps", "t_ps", "m_ps"))
        o_ps, r_ps = (psum(n, [P, N]) for n in ("o_ps", "r_ps"))

        w_loaded, w_upper, w_split = sem("w_loaded"), sem("w_upper"), sem("w_split")
        consts, consts_in = sem("consts"), sem("consts_in")
        x_loaded, adj_loaded, x_stored = ([sem(f"{n}{s}") for s in range(2)]
                                          for n in ("x_loaded", "adj_loaded", "x_stored"))
        stacked = [[sem(f"stacked{s}{j}") for j in range(GH)] for s in range(2)]
        scores_done, masked_done, probs_done, turned = (
            sem(n) for n in ("scores_done", "masked_done", "probs_done", "turned"))
        hi_done, lo_done, weighed = (sem(n) for n in ("hi_done", "lo_done", "weighed"))
        out_copied, out_turned, out_normed, rsum_done = (
            sem(n) for n in ("out_copied", "out_turned", "out_normed", "rsum_done"))
        stat_done, mv_done, ln_steps, h_done = (sem(n) for n in ("stat_done", "mv_done", "ln_steps", "h_done"))
        made = {k: sem(f"{k}_made") for k in ("turn_h", "qk", "value", "turn_a", "project")}
        upper = {k: sem(f"{k}_upper") for k in ("turn_h", "qk", "value", "turn_a")}
        taken = {k: sem(f"{k}_taken") for k in ("turn_h", "qk", "value", "turn_a", "project")}
        per = {"turn_h": T, "qk": 2 * G, "value": T, "turn_a": T, "project": T}
        if first:
            bias_steps, bias_done, updated = sem("bias_steps"), sem("bias_done"), sem("updated")
        else:
            halved, folded, total_done, size_done, kept_done = (
                sem(n) for n in ("halved", "folded", "total_done", "size_done", "kept_done"))
        LN_STEPS = 9

        def bank_of(step, kind, k):
            return [t[:3] for t in side].index((step, kind, k)) % 2

        def bank_free(eng, graph, step, kind, k):
            at = [t[:3] for t in side].index((step, kind, k)) - 2
            while True:
                _, kind0, k0, off = side[at % len(side)]
                g0 = Graph(graph.c + off + at // len(side), graph.i)
                if g0.c < -1 and g0.i is None:
                    return
                if g0.exists():
                    wait(eng, taken[kind0], g0.count(per[kind0], k0 + 1))
                    return
                at -= 2
                if at < -2 * len(side):
                    return

        def own_tasks(step, graph):
            return [(kind, k, Graph(graph.c + off, graph.i)) for s, kind, k, off in side
                    if s == step and Graph(graph.c + off, graph.i).exists()]

        def tile_of(step, graph, lag):
            n, g = step - lag, graph
            while n < 0:
                n, g = n + STEPS, g.prev()
            return (g, n) if n < STEPS and g.exists() else None

        def pair_of(step, graph, lag):
            at = tile_of(step, graph, lag)
            if at and at[1] % (2 * T) == T:
                return at[0], at[1] // (2 * T)
            return None

        def walk(eng, head, job):
            head(Graph(0))
            job(Graph(0), range(STEPS))
            with eng.Fori(0, (B - 2) // 2) as i:
                job(Graph(1, i), range(STEPS))
                job(Graph(2, i), range(STEPS))
            job(Graph(B - 1), range(STEPS))
            job(Graph(B), range(TAIL + (0 if first else 12)))

        block = ctx.enter_context(nc.Block())

        @block.sync
        def _(sp):
            def load_adj(g):
                wait(sp, masked_done, g.prev().count(STEPS, 0))
                sp.dma_start(bias[:, g.slot()], adj[g.number()].rearrange("(t p) n -> p t n", p=P)
                             ).then_inc(adj_loaded[g.slot()], 16)

            def load_x(g):
                if g.i is not None or g.c >= 2:
                    wait(sp, x_stored[g.slot()], g.slot_count(16) - 16)
                sp.dma_start(x_sb[:, g.slot()], x_in[g.number()].rearrange("(t p) d -> p t d", p=P)
                             ).then_inc(x_loaded[g.slot()], 16)

            def store_x(g):
                if first:
                    wait(sp, updated, g.count(PAIRS, PAIRS))
                else:
                    wait(sp, taken["project"], g.count(T, T))
                sp.dma_start(x_out[g.number()].rearrange("(t p) d -> p t d", p=P), x_sb[:, g.slot()]
                             ).then_inc(x_stored[g.slot()], 16)

            def stack(g, grp):
                slot = g.group_slot(grp)
                for which, dst, order in ((0, q_stack, (qk_hi, qk_hi, qk_lo)), (1, k_stack, (qk_hi, qk_lo, qk_hi))):
                    wait(sp, taken["qk"], g.count(2 * G, 2 * grp + which + 1))
                    for j in range(GH):
                        for r, src in enumerate(order):
                            sp.dma_start(dst[r * HD:(r + 1) * HD, slot, j, :].bitcast(F32),
                                         src[j * HD:(j + 1) * HD, which, :].bitcast(F32)
                                         ).then_inc(stacked[slot][j], 16)

            sp.dma_start(x_sb[:, 0], x_in[0].rearrange("(t p) d -> p t d", p=P)).then_inc(x_loaded[0], 16)
            for n, name in enumerate(names):
                wait(sp, w_split, n)
                sp.dma_start(w_raw[:], w_in[name].rearrange("(c p) n -> p c n", p=P)).then_inc(w_loaded, 16)
                if n == 0:
                    sp.dma_start(row_raw[:], b_in["v"].unsqueeze(0)).then_inc(consts_in, 16)
                    if first:
                        sp.dma_start(qk_bias[:, 0, :], b_in["q"].rearrange("(g p) -> p g", p=P),
                                     allow_slow_non_contiguous=True).then_inc(consts_in, 16)
                        sp.dma_start(qk_bias[:, 1, :], b_in["k"].rearrange("(g p) -> p g", p=P),
                                     allow_slow_non_contiguous=True).then_inc(consts_in, 16)
                        sp.dma_start(beta_col[:], beta.partition_broadcast(P)).then_inc(consts_in, 16)
            sp.dma_start(bias[:, 0], adj[0].rearrange("(t p) n -> p t n", p=P)).then_inc(adj_loaded[0], 16)
            if not first:
                sp.wait_ge(w_split, len(names) + 1)
                sp.dma_start(row_raw[:], b_in["o"].unsqueeze(0)).then_inc(consts_in, 16)

            def job(g, steps):
                if not g.exists():
                    store_x(g.prev())
                    return
                if g.next().exists():
                    load_adj(g.next())
                if g.c == 0 and g.i is None:
                    load_x(g.next())
                stack(g, 1)
                if g.prev().exists():
                    store_x(g.prev())
                    if g.next().exists():
                        load_x(g.next())
                stack(g, 2)
                if g.next().exists():
                    stack(g.next(), 0)

            walk(sp, lambda g: stack(g, 0), job)
            for s in range(2):
                sp.wait_ge(x_stored[s], 16 * B // 2)

        @block.gpsimd
        def _(pool):
            nc.gpsimd.memset(ident[:], 0.0)
            nc.gpsimd.memset(fold[:], 0.0)
            nc.gpsimd.memset(one_rows[:].bitcast(F32), 0.0)
            nc.gpsimd.memset(v_row[:].bitcast(F32), 0.0)
            if not first:
                nc.gpsimd.memset(o_row[:].bitcast(F32), 0.0)
            nc.gpsimd.memset(eps[:], EPS)
            nc.gpsimd.memset(neg_half[:], -0.5)
            nc.gpsimd.memset(one_half[:], 1.5)
            nc.gpsimd.memset(v_stack[:].bitcast(F32), 0.0).then_inc(consts, 1)
            pool.wait_ge(consts, 1)
            nc.gpsimd.memset(one_rows[0:1, :].bitcast(F32), 1.0).then_inc(consts, 1)
            pool.wait_ge(consts, 2)
            nc.gpsimd.memset(one_rows[HD:HD + 1, :].bitcast(F32), 1.0).then_inc(consts, 1)
            pool.wait_ge(consts, 3)
            nc.gpsimd.affine_select(out=ident[:], in_=ident[:], compare_op=ALU.not_equal, fill=1.0, base=0,
                                    pattern=[[-1, P]], channel_multiplier=1).then_inc(consts, 1)
            for r in range(2):
                view = fold[:].rearrange("p (b c) -> p b c", b=2)
                nc.gpsimd.affine_select(out=view, in_=view, compare_op=ALU.not_equal, fill=1.0, base=-HD * r,
                                        pattern=[[-2 * HD, 2], [-1, HD]], channel_multiplier=1
                                        ).then_inc(consts, 1)
                pool.wait_ge(consts, 5 + r)

            def inverse_deviation(g):
                pool.wait_ge(mv_done, g.count(1, 1))
                wait(pool, h_done, g.count(T, 0))
                nc.gpsimd.tensor_tensor(var_eps[:], mean_var[:, :, 1], eps[:], ALU.add).then_inc(ln_steps, 1)
                pool.wait_ge(ln_steps, g.count(LN_STEPS, 1))
                nc.gpsimd.tensor_tensor(root0[:], var_eps[:], neg_half[:], ALU.pow).then_inc(ln_steps, 1)
                pool.wait_ge(ln_steps, g.count(LN_STEPS, 2))
                nc.gpsimd.tensor_tensor(sq[:], root0[:], root0[:], ALU.mult).then_inc(ln_steps, 1)
                nc.gpsimd.tensor_tensor(half_var[:], var_eps[:], neg_half[:], ALU.mult).then_inc(ln_steps, 1)
                nc.gpsimd.tensor_scalar(neg_mean[:], mean_var[:, :, 0], -1.0, None, ALU.mult).then_inc(ln_steps, 1)
                pool.wait_ge(ln_steps, g.count(LN_STEPS, 5))
                nc.gpsimd.tensor_tensor(prod[:], sq[:], half_var[:], ALU.mult).then_inc(ln_steps, 1)
                pool.wait_ge(ln_steps, g.count(LN_STEPS, 6))
                nc.gpsimd.tensor_tensor(fix[:], prod[:], one_half[:], ALU.add).then_inc(ln_steps, 1)
                pool.wait_ge(ln_steps, g.count(LN_STEPS, 7))
                nc.gpsimd.tensor_tensor(rstd[:], root0[:], fix[:], ALU.mult).then_inc(ln_steps, 1)
                pool.wait_ge(ln_steps, g.count(LN_STEPS, 8))
                nc.gpsimd.tensor_tensor(shift[:], neg_mean[:], rstd[:], ALU.mult).then_inc(ln_steps, 1)

            def make_bias(g, t):
                tile = bias[:, g.slot(), t, :]
                if t == 0:
                    pool.wait_ge(adj_loaded[g.slot()], g.slot_count(16))
                wait(pool, bias_done, g.count(T, t))
                nc.gpsimd.tensor_tensor(scaled[:], tile, beta_col[:].broadcast_to([P, N]), ALU.mult
                                        ).then_inc(bias_steps, 1)
                nc.gpsimd.tensor_scalar(hole[:], tile, 0.0, MASKED, ALU.is_le, ALU.mult).then_inc(bias_steps, 1)
                pool.wait_ge(bias_steps, g.count(2 * T, 2 * t + 2))
                nc.gpsimd.tensor_tensor(tile, scaled[:], hole[:], ALU.add).then_inc(bias_done, 1)

            def update_x(g, p):
                pool.wait_ge(out_normed, g.count(PAIRS, p + 1))
                cols = x_sb[:, g.slot(), :, p * 2 * HD:(p + 1) * 2 * HD]
                nc.gpsimd.tensor_tensor(cols, cols, update[:, p % 2], ALU.add).then_inc(updated, 1)

            def total_of(g, n):
                u, t = n // T, n % T
                pool.wait_ge(masked_done, g.count(STEPS, n + 1))
                if t == 0:
                    wait(pool, total_done, g.count(H, u - 1))
                nc.gpsimd.tensor_tensor(halves[:, u % 2, t, :], masked[:, n % 4, 0:N // 2],
                                        masked[:, n % 4, N // 2:N], ALU.add).then_inc(halved, 1)
                if t == T - 1:
                    pool.wait_ge(halved, g.count(STEPS, n + 1))
                    for level, w in enumerate((N // 4, N // 8, N // 16)):
                        nc.gpsimd.tensor_tensor(halves[:, u % 2, :, 0:w], halves[:, u % 2, :, 0:w],
                                                halves[:, u % 2, :, w:2 * w], ALU.add).then_inc(folded, 1)
                        pool.wait_ge(folded, g.count(3 * H, 3 * u + level + 1))

            def head(g):
                if first:
                    pool.wait_ge(consts_in, 16 * 4)
                    for t in range(T):
                        make_bias(g, t)
                inverse_deviation(g)

            def job(g, steps):
                for step in steps:
                    if not first and g.exists():
                        total_of(g, step)
                    if first and g.next().exists() and step in (9, 13, 27, 35):
                        make_bias(g.next(), (9, 13, 27, 35).index(step))
                    if step == stats_step + 2 and g.exists() and g.next().exists():
                        inverse_deviation(g.next())
                    at = pair_of(step, g, LAG_NORM)
                    if first and at:
                        update_x(*at)

            walk(pool, head, job)

        @block.scalar
        def _(act):
            def apply_norm(g, t):
                if t == 0:
                    act.wait_ge(ln_steps, g.count(LN_STEPS, LN_STEPS))
                wait(act, made["turn_h"], g.count(T, max(t - 1, 0)))
                nc.scalar.activation(h[:, t % 2, :], x_sb[:, g.slot(), t, :], ACT.Relu, bias=shift[:, t:t + 1],
                                     scale=rstd[:, t:t + 1]).then_inc(h_done, 1)

            def upper_part(kind, k, g, bank):
                act.wait_ge(made[kind], g.count(per[kind], k + 1))
                if kind == "turn_h":
                    nc.scalar.activation(ht_hi[:, :, k * P:(k + 1) * P],
                                         m_ps[:, bank, 0:D].rearrange("p (c n) -> p c n", c=C),
                                         ACT.Copy).then_inc(upper[kind], 1)
                elif kind == "turn_a":
                    nc.scalar.activation(at_hi[:, k % 2], m_ps[:, bank, 0:D].rearrange("p (c n) -> p c n", c=C),
                                         ACT.Copy).then_inc(upper[kind], 1)
                elif kind == "value":
                    nc.scalar.activation(v_stack[:, k, :, 0:3:2, 0:HD],
                                         m_ps[:, bank, 0:D].rearrange("p (a b d) -> p a b d", b=2, d=HD),
                                         ACT.Copy).then_inc(upper[kind], 1)
                elif kind == "qk":
                    grp, which = k // 2, k % 2
                    if which == 0 and not (g.i is None and g.c == 0 and grp == 0):
                        for j in range(GH):
                            act.wait_ge(stacked[1 - g.group_slot(grp)][j], g.group_count(grp, 16 * STACKS, 1))
                    if first:
                        nc.scalar.activation(qk_hi[:, which, :], m_ps[:, bank, :], ACT.Identity,
                                             bias=qk_bias[:, which, grp:grp + 1]).then_inc(upper[kind], 1)
                    else:
                        nc.scalar.activation(qk_hi[:, which, :], m_ps[:, bank, :], ACT.Copy).then_inc(upper[kind], 1)

            for n, name in enumerate(names):
                act.wait_ge(w_loaded, 16 * (n + 1))
                nc.scalar.activation(w_hi[name][:], w_raw[:], ACT.Copy, scale=scale[name]).then_inc(w_upper, 1)
            act.wait_ge(consts_in, 16 * (4 if first else 1))
            act.wait_ge(consts, 1)
            nc.scalar.activation(v_row[0:1, :], row_raw[:], ACT.Copy).then_inc(w_upper, 1)
            if not first:
                act.wait_ge(consts_in, 32)
                nc.scalar.activation(o_row[0:1, :], row_raw[:], ACT.Copy).then_inc(w_upper, 1)

            def head(g):
                for t in range(T):
                    apply_norm(g, t)
                    upper_part("turn_h", t, g, bank_of(side_at("turn_h", t), "turn_h", t))
                for k in range(2):
                    upper_part("qk", k, g, bank_of(side_at("qk", k), "qk", k))

            def side_at(kind, k):
                return [s for s, kk, n, _ in side if (kk, n) == (kind, k)][0]

            def job(g, steps):
                for step in steps:
                    for kind, k, of in own_tasks(step - 1, g):
                        upper_part(kind, k, of, bank_of(step - 1, kind, k)) if kind != "project" else None
                    for kind, k, of in own_tasks(step + 1, g):
                        if kind == "turn_h":
                            apply_norm(of, k)
                    at = pair_of(step, g, LAG_COPY)
                    if at:
                        act.wait_ge(weighed, at[0].count(STEPS, (2 * at[1] + 2) * T))
                        wait(act, out_turned, at[0].count(PAIRS, at[1]))
                        nc.scalar.activation(out_t[:], o_ps[:], ACT.Copy).then_inc(out_copied, 1)
                    at = tile_of(step, g, LAG_TURN)
                    if at:
                        of, n = at
                        u, t = n // T, n % T
                        act.wait_ge(turned, of.count(STEPS, n + 1))
                        if t == 0:
                            wait(act, weighed, of.count(STEPS, (u - 1) * T))
                        nc.scalar.activation(pt_hi[:, u % 2, :, t * P:(t + 1) * P],
                                             t_ps[:, n % 2, :].rearrange("p (c q) -> p c q", c=T),
                                             ACT.Copy).then_inc(hi_done, 1)
                    if g.exists():
                        n = step
                        u, t = n // T, n % T
                        act.wait_ge(masked_done, g.count(STEPS, n + 1))
                        wait(act, turned, g.count(STEPS, n - 3))
                        if n == 0 and g.prev().exists():
                            act.wait_ge(rsum_done, g.prev().count(PAIRS, 1))
                        nc.scalar.activation(probs[:, n % 4, :], masked[:, n % 4, :], ACT.Exp,
                                             bias=neg_max[:, g.slot(), u, t:t + 1], scale=-1.0,
                                             accum_out=sums[:, g.slot(), u, t:t + 1]).then_inc(probs_done, 1)

            walk(act, head, job)

        @block.vector
        def _(dve):
            def lower_part(kind, k, g, bank):
                if kind == "project":
                    dve.wait_ge(made[kind], g.count(T, k + 1))
                    row = x_sb[:, g.slot(), k, :]
                    nc.vector.tensor_tensor(row, m_ps[:, bank, 0:D], row, ALU.add).then_inc(taken[kind], 1)
                    return
                dve.wait_ge(upper[kind], g.count(per[kind], k + 1))
                if kind == "turn_h":
                    cols = slice(k * P, (k + 1) * P)
                    nc.vector.tensor_tensor(ht_lo[:, :, cols], m_ps[:, bank, 0:D].rearrange("p (c n) -> p c n", c=C),
                                            ht_hi[:, :, cols].bitcast(F32), ALU.subtract).then_inc(taken[kind], 1)
                elif kind == "turn_a":
                    nc.vector.tensor_tensor(at_lo[:, k % 2], m_ps[:, bank, 0:D].rearrange("p (c n) -> p c n", c=C),
                                            at_hi[:, k % 2].bitcast(F32), ALU.subtract).then_inc(taken[kind], 1)
                elif kind == "value":
                    nc.vector.tensor_tensor(v_stack[:, k, :, 0:3:2, HD:2 * HD],
                                            m_ps[:, bank, 0:D].rearrange("p (a b d) -> p a b d", b=2, d=HD),
                                            v_stack[:, k, :, 0:3:2, 0:HD].bitcast(F32), ALU.subtract
                                            ).then_inc(taken[kind], 1)
                elif kind == "qk":
                    grp, which = k // 2, k % 2
                    if first:
                        nc.vector.scalar_tensor_tensor(out=qk_lo[:, which, :], in0=m_ps[:, bank, :],
                                                       scalar=qk_bias[:, which, grp:grp + 1],
                                                       in1=qk_hi[:, which, :].bitcast(F32), op0=ALU.add,
                                                       op1=ALU.subtract).then_inc(taken[kind], 1)
                    else:
                        nc.vector.tensor_tensor(qk_lo[:, which, :], m_ps[:, bank, :],
                                                qk_hi[:, which, :].bitcast(F32), ALU.subtract
                                                ).then_inc(taken[kind], 1)

            def statistics(g):
                dve.wait_ge(x_loaded[g.slot()], g.slot_count(16))
                for t in range(T):
                    nc.vector.bn_stats(stat[:, t, :], x_sb[:, g.slot(), t, :]).then_inc(stat_done, 1)

            def moments_wait(g):
                dve.wait_ge(stat_done, g.count(T, T))
                wait(dve, ln_steps, g.count(LN_STEPS, 0))

            def moments():
                for t in range(T):
                    last = nc.vector.bn_aggr(mean_var[:, t, :], stat[:, t, :])
                last.then_inc(mv_done, 1)

            for n, name in enumerate(names):
                dve.wait_ge(w_upper, n + 1)
                nc.vector.scalar_tensor_tensor(out=w_lo[name][:].rearrange("p c n -> p (c n)"),
                                               in0=w_raw[:].rearrange("p c n -> p (c n)"), scalar=scale[name],
                                               in1=w_hi[name][:].rearrange("p c n -> p (c n)").bitcast(F32),
                                               op0=ALU.mult, op1=ALU.subtract).then_inc(w_split, 1)
            if first:
                nc.vector.tensor_scalar(qk_bias[:, 0, :], qk_bias[:, 0, :], scale["q"], None, ALU.mult
                                        ).then_inc(w_split, 1)
            dve.wait_ge(w_upper, len(names) + 1)
            nc.vector.tensor_tensor(v_row[HD:HD + 1, :], row_raw[:], v_row[0:1, :].bitcast(F32), ALU.subtract
                                    ).then_inc(w_split, 1)
            if not first:
                dve.wait_ge(w_upper, len(names) + 2)
                nc.vector.tensor_tensor(o_row[HD:HD + 1, :], row_raw[:], o_row[0:1, :].bitcast(F32),
                                        ALU.subtract).then_inc(w_split, 1)

            def side_at(kind, k):
                return [s for s, kk, n, _ in side if (kk, n) == (kind, k)][0]

            def head(g):
                statistics(g)
                moments_wait(g)
                moments()
                for t in range(T):
                    lower_part("turn_h", t, g, bank_of(side_at("turn_h", t), "turn_h", t))
                for k in range(2):
                    lower_part("qk", k, g, bank_of(side_at("qk", k), "qk", k))
                if first:
                    dve.wait_ge(bias_done, T)
                else:
                    dve.wait_ge(adj_loaded[0], 16)

            def out_rows(g, p, stage):
                sl = g.slot()
                mine = slice(2 * p, 2 * p + 2)
                if stage == 0:
                    dve.wait_ge(probs_done, g.count(STEPS, (2 * p + 2) * T))
                    wait(dve, out_normed, g.count(PAIRS, p - 1))
                    nc.vector.reciprocal(rsum[:, p % 2], sums[:, sl, mine, :]).then_inc(rsum_done, 1)
                    if not first:
                        dve.wait_ge(total_done, g.count(H, 2 * p + 2))
                        wait(dve, kept_done, g.count(PAIRS, p))
                        nc.vector.scalar_tensor_tensor(
                            out=size[:].rearrange("p h t -> p (h t)"),
                            in0=neg_max[:, sl, mine, :].rearrange("p h t -> p (h t)"), scalar=0.0,
                            in1=total[:, sl, mine, :].rearrange("p h t -> p (h t)"), op0=ALU.not_equal, op1=ALU.max
                        ).then_inc(size_done, 1)
                elif stage == 1 and not first:
                    dve.wait_ge(size_done, g.count(PAIRS, p + 1))
                    dve.wait_ge(rsum_done, g.count(PAIRS, p + 1))
                    nc.vector.scalar_tensor_tensor(
                        out=kept[:, p % 2].rearrange("p h t -> p (h t)"), in0=size[:].rearrange("p h t -> p (h t)"),
                        scalar=0.0, in1=rsum[:, p % 2].rearrange("p h t -> p (h t)"), op0=ALU.is_gt, op1=ALU.mult
                    ).then_inc(kept_done, 1)
                elif stage == 2:
                    dve.wait_ge(out_turned, g.count(PAIRS, p + 1))
                    factor = rsum if first else kept
                    if first:
                        dve.wait_ge(rsum_done, g.count(PAIRS, p + 1))
                        wait(dve, updated, g.count(PAIRS, p - 1))
                        out = update[:, p % 2].rearrange("p t (h d) -> p t h d", h=2)
                    else:
                        dve.wait_ge(kept_done, g.count(PAIRS, p + 1))
                        if p == 0:
                            wait(dve, made["turn_a"], g.count(T, 0))
                        out = attn[:, :, p * 2 * HD:(p + 1) * 2 * HD].rearrange("p t (h d) -> p t h d", h=2)
                    by = factor[:, p % 2].rearrange("p h t -> p t h").unsqueeze(3).broadcast_to([P, T, 2, HD])
                    nc.vector.tensor_tensor(out, r_ps[:, 0:N // 2].rearrange("p (t h d) -> p t h d", t=T, h=2), by,
                                            ALU.mult).then_inc(out_normed, 1)

            def job(g, steps):
                for step in steps:
                    tasks = own_tasks(step - 2, g)
                    for kind, k, of in tasks:
                        lower_part(kind, k, of, bank_of(step - 2, kind, k))
                    if g.exists() and g.next().exists():
                        if step == stats_step:
                            statistics(g.next())
                        if step == stats_step + 1:
                            moments_wait(g.next())
                    for stage, lag in enumerate((LAG_COPY, LAG_OUT, LAG_NORM)):
                        at = pair_of(step, g, lag)
                        if at:
                            out_rows(*at, stage)
                    if not first:
                        at = tile_of(step, g, T + 1)
                        if at and at[1] % T == 0:
                            of, u = at[0], at[1] // T
                            dve.wait_ge(folded, of.count(3 * H, 3 * u + 3))
                            nc.vector.tensor_reduce(total[:, of.slot(), u, :], halves[:, u % 2, :, 0:N // 16], AX.X,
                                                    ALU.add).then_inc(total_done, 1)
                    if g.exists():
                        n = step
                        dve.wait_ge(scores_done, g.count(STEPS, n + 1))
                        if n == 0 and not (g.i is None and g.c == 0):
                            if first:
                                dve.wait_ge(bias_done, g.count(T, T))
                            else:
                                dve.wait_ge(adj_loaded[g.slot()], g.slot_count(16))
                        wait(dve, probs_done, g.count(STEPS, n - 3))
                        if not first:
                            wait(dve, halved, g.count(STEPS, n - 3))
                    at = tile_of(step, g, LAG_LO)
                    if at:
                        of, n = at
                        u, t = n // T, n % T
                        dve.wait_ge(hi_done, of.count(STEPS, n + 1))
                        dst = (slice(None), u % 2, slice(None), slice(t * P, (t + 1) * P))
                        nc.vector.tensor_tensor(pt_lo[dst], t_ps[:, n % 2, :].rearrange("p (c q) -> p c q", c=T),
                                                pt_hi[dst].bitcast(F32), ALU.subtract).then_inc(lo_done, 1)
                    if g.exists():
                        n = step
                        u, t = n // T, n % T
                        nc.vector.tensor_tensor_reduce(
                            out=masked[:, n % 4, :], in0=s_ps[:, n % 2, :], in1=bias[:, g.slot(), t, :], scale=negate,
                            scalar=BIG, op0=ALU.add, op1=ALU.min, accum_out=neg_max[:, g.slot(), u, t:t + 1]
                        ).then_inc(masked_done, 1)
                        if step == stats_step + 1 and g.next().exists():
                            moments()

            walk(dve, head, job)

        @block.tensor
        def _(pe):
            def three_passes(out, a_hi, a_lo, b_hi, b_lo, rows, row=None):
                terms = [(a, b, c) for c in range(C) for a, b in ((a_hi, b_hi), (a_hi, b_lo), (a_lo, b_hi))]
                for n, (a, b, c) in enumerate(terms):
                    last = nc.tensor.matmul(out, a[c], b[c], start=n == 0, stop=row is None and n == len(terms) - 1)
                if row is not None:
                    last = nc.tensor.matmul(out, one_rows[:], row[:], start=False, stop=True)
                return last

            def make(kind, k, g, step):
                bank = bank_of(step, kind, k)
                out = m_ps[:, bank, :]
                sched = Graph(g.c - [t[3] for t in side if t[1:3] == (kind, k)][0], g.i)
                bank_free(pe, sched, step, kind, k)
                if kind == "turn_h":
                    pe.wait_ge(h_done, g.count(T, k + 1))
                    for c in range(C):
                        last = nc.tensor.transpose(out[:, c * P:(c + 1) * P], h[:, k % 2, c * P:(c + 1) * P], ident[:])
                elif kind == "turn_a":
                    pe.wait_ge(out_normed, g.count(PAIRS, PAIRS))
                    for c in range(C):
                        last = nc.tensor.transpose(out[:, c * P:(c + 1) * P], attn[:, k, c * P:(c + 1) * P], ident[:])
                elif kind == "project":
                    pe.wait_ge(taken["turn_a"], g.count(T, k + 1))
                    last = three_passes(out[:, 0:D], [at_hi[:, k % 2, c, :] for c in range(C)],
                                        [at_lo[:, k % 2, c, :] for c in range(C)],
                                        [w_hi["o"][:, c, :] for c in range(C)], [w_lo["o"][:, c, :] for c in range(C)],
                                        C, o_row)
                elif kind == "value":
                    pe.wait_ge(taken["turn_h"], g.count(T, T))
                    cols = slice(k * P, (k + 1) * P)
                    last = three_passes(out[:, 0:D], [ht_hi[:, c, cols] for c in range(C)],
                                        [ht_lo[:, c, cols] for c in range(C)],
                                        [w_hi["v"][:, c, :] for c in range(C)], [w_lo["v"][:, c, :] for c in range(C)],
                                        C, v_row)
                elif kind == "qk":
                    pe.wait_ge(taken["turn_h"], g.count(T, T))
                    grp, name = k // 2, "qk"[k % 2]
                    cols = slice(grp * P, (grp + 1) * P)
                    last = three_passes(out, [w_hi[name][:, c, cols] for c in range(C)],
                                        [w_lo[name][:, c, cols] for c in range(C)],
                                        [ht_hi[:, c, :] for c in range(C)], [ht_lo[:, c, :] for c in range(C)], C)
                last.then_inc(made[kind], 1)

            pe.wait_ge(consts, 6)
            pe.wait_ge(w_split, len(names) + 2)

            def side_at(kind, k):
                return [s for s, kk, n, _ in side if (kk, n) == (kind, k)][0]

            def head(g):
                for t in range(T):
                    make("turn_h", t, g, side_at("turn_h", t))
                for k in range(2):
                    make("qk", k, g, side_at("qk", k))

            def job(g, steps):
                for step in steps:
                    if g.exists():
                        n = step
                        u, t = n // T, n % T
                        grp, j = u // GH, u % GH
                        slot = g.group_slot(grp)
                        if t == 0:
                            pe.wait_ge(stacked[slot][j], g.group_count(grp, 16 * STACKS))
                        wait(pe, masked_done, g.count(STEPS, n - 1))
                        nc.tensor.matmul(s_ps[:, n % 2, :], q_stack[:, slot, j, t * P:(t + 1) * P],
                                         k_stack[:, slot, j, :], start=True, stop=True).then_inc(scores_done, 1)
                    at = tile_of(step, g, LAG_TURN)
                    if at:
                        of, n = at
                        pe.wait_ge(probs_done, of.count(STEPS, n + 1))
                        wait(pe, lo_done, of.count(STEPS, n - 1))
                        for c in range(T):
                            last = nc.tensor.transpose(t_ps[:, n % 2, c * P:(c + 1) * P],
                                                       probs[:, n % 4, c * P:(c + 1) * P], ident[:])
                        last.then_inc(turned, 1)
                    at = pair_of(step, g, LAG_OUT)
                    if at:
                        of, p = at
                        pe.wait_ge(out_copied, of.count(PAIRS, p + 1))
                        wait(pe, out_normed, of.count(PAIRS, p))
                        for t in range(T):
                            last = nc.tensor.matmul(r_ps[:, t * 2 * HD:(t + 1) * 2 * HD], out_t[:, t * P:(t + 1) * P],
                                                    fold[:], start=True, stop=True)
                        last.then_inc(out_turned, 1)
                    at = tile_of(step, g, LAG_WEIGH)
                    if at:
                        of, n = at
                        u, c = n // T, n % T
                        if c == 0:
                            pe.wait_ge(lo_done, of.count(STEPS, (u + 1) * T))
                            if u % 2 == 0:
                                wait(pe, out_copied, of.count(PAIRS, u // 2))
                        if u == 0:
                            pe.wait_ge(taken["value"], of.count(T, c + 1))
                        values = v_stack[:, c, u // 2].rearrange("p a b -> p (a b)")
                        values = values[:, 0:P] if u % 2 == 0 else values[:, 2 * HD:2 * HD + P]
                        nc.tensor.matmul(o_ps[:], values, pt_hi[:, u % 2, c, :], start=u % 2 == 0 and c == 0,
                                         stop=False)
                        nc.tensor.matmul(o_ps[:], values, pt_lo[:, u % 2, c, :], start=False,
                                         stop=u % 2 == 1 and c == T - 1).then_inc(weighed, 1)
                    for kind, k, of in own_tasks(step, g):
                        make(kind, k, of, step)

            walk(pe, head, job)


def graph_attention_kernel(nc, x, adj, q0, bq0, k0, bk0, v0, bv0, beta, q1, k1, v1, bv1, o1, bo1, out):
    between = nc.dram_tensor("between_dram", (B, N, D), F32, kind="Internal").ap()
    layer_pass(nc, 0, x, adj, {"q": q0, "k": k0, "v": v0}, {"q": bq0, "k": bk0, "v": bv0}, beta, between)
    layer_pass(nc, 1, between, adj, {"q": q1, "k": k1, "v": v1, "o": o1}, {"v": bv1, "o": bo1}, None, out)


def kernel(**inputs):
    import numpy as _np
    import concourse.bacc as _bacc
    from concourse import mybir as _mybir
    from concourse.bass_utils import run_bass_kernel_spmd as _run

    nc = _bacc.Bacc("TRN2", target_bir_lowering=False, num_devices=1, dynamic_dma_scratch_size=1024)
    names = ["x", "adj", "L0_gnn_Wq", "L0_gnn_bq", "L0_gnn_Wk", "L0_gnn_bk", "L0_gnn_Wv", "L0_gnn_bv",
             "L0_gnn_beta", "L1_gnn_Wq", "L1_gnn_Wk", "L1_gnn_Wv", "L1_gnn_bv", "L1_gnn_Wo", "L1_gnn_bo"]
    transposed = {"L1_gnn_Wq", "L1_gnn_Wk", "L1_gnn_Wv", "L1_gnn_Wo"}
    arrays, args = {}, []
    for name in names:
        a = _np.asarray(inputs[name])
        a = a.T if name in transposed else a
        a = _np.ascontiguousarray(a.reshape(1) if a.ndim == 0 else a)
        arrays[f"in_{name}_dram"] = a
        args.append(nc.dram_tensor(f"in_{name}_dram", a.shape, _mybir.dt.from_np(a.dtype), kind="ExternalInput").ap())
    out = nc.dram_tensor("out_dram", (16, 512, 384), _mybir.dt.float32, kind="ExternalOutput").ap()
    graph_attention_kernel(nc, *args, out)
    r = _run(nc, [arrays], core_ids=[0])
    return r.results[0]["out_dram"]
```

```python
from contextlib import ExitStack

import concourse.bass as bass
from concourse import mybir
import numpy as np

F32 = mybir.dt.float32
F32R = mybir.dt.float32r
ALU = mybir.AluOpType
ACT = mybir.ActivationFunctionType
AX = mybir.AxisListType

B, N, D, H = 16, 512, 384, 12
HD = D // H
P = 128
T = N // P
C = D // P
GH = P // HD
G = H // GH
STEPS = H * T
PAIRS = H // 2
EPS = 1e-5
MASKED = -9000000000000000.0
BIG = 3.0e38
SPLIT_ROWS = 3 * HD
STACKS = 3

BIAS_STEPS = (5, 19, 27, 35)
LAG_TURN = 2
LAG_LO = 3
LAG_TOTAL = T + 2
LAG_WEIGH = ((8, 8, 9, 10), (7, 8, 9, 10))
LAG_COPY, LAG_OUT, LAG_NORM = T + 7, T + 8, T + 9


class Graph:

    def __init__(self, c, i=None):
        self.c, self.i = c, i

    def next(self):
        return Graph(self.c + 1, self.i)

    def prev(self):
        return Graph(self.c - 1, self.i)

    def exists(self):
        return self.i is not None or 0 <= self.c < B

    def slot(self):
        return self.c % 2

    def number(self):
        return self.c if self.i is None else self.i * 2 + self.c

    def count(self, per_graph, more):
        c = self.c * per_graph + more
        assert self.i is None or c > 0, "a wait on zero"
        return c if self.i is None else self.i * (2 * per_graph) + c

    def slot_count(self, by):
        c = by * (self.c // 2 + 1)
        return c if self.i is None else self.i * by + c

    def group_slot(self, g):
        return (G * self.c + g) % 2

    def group_count(self, g, by, back=0):
        c = by * ((G * self.c + g - back) // 2 + 1)
        return c if self.i is None else self.i * (G * by) + c


def wait(eng, sem, value):
    if not isinstance(value, int) or value > 0:
        eng.wait_ge(sem, value)


def side_tasks(layer):
    tasks = []

    def add(kind, k, off, start, parts=1):
        tasks.append((tuple(range(start, start + parts)), kind, k, off))

    for p in range(PAIRS):
        step = 2 * T * p + T + LAG_OUT
        add("turn_out", p, -(step // STEPS), step % STEPS)
    for t in range(T):
        add("value", t, 0, 3 + t)
    add("qk", 2, 0, 0, 3)
    add("qk", 3, 0, 7, 3)
    if layer == 0:
        add("qk", 4, 0, 16, 4)
        add("qk", 5, 0, 20, 5)
        for t in range(T):
            add("turn_h", t, 1, (25, 27, 28, 30)[t])
        add("qk", 0, 1, 31, 5)
        add("qk", 1, 1, 36, 5)
    else:
        for t in range(T):
            add("turn_a", t, -1, 11 + t)
        add("qk", 4, 0, 16, 4)
        add("qk", 5, 0, 20, 3)
        add("project", 0, -1, 23, 3)
        add("turn_h", 0, 1, 26)
        add("turn_h", 1, 1, 27)
        add("project", 1, -1, 28, 3)
        add("turn_h", 2, 1, 31)
        add("turn_h", 3, 1, 33)
        add("project", 2, -1, 34, 3)
        add("project", 3, -1, 36, 3)
        add("qk", 0, 1, 39, 3)
        add("qk", 1, 1, 41, 3)
    tasks.sort()
    end, placed = [-2, -1], []
    for steps, kind, k, off in tasks:
        bank = end.index(min(end))
        assert steps[0] > end[bank]
        end[bank] = steps[-1]
        placed.append((steps, kind, k, off, bank))
    return placed


def layer_pass(nc, layer, x_in, adj, w_in, b_in, beta, x_out):
    first = layer == 0
    side = side_tasks(layer)
    stats_steps = (10, 11, 13, 14) if first else (10, 18, 19, 21)
    moments_step = stats_steps[-1] + 1
    tail = max(LAG_NORM, *(steps[-1] + 2 for steps, _, _, off, _ in side if off < 0)) + 1
    names = ["q", "k", "v"] + ([] if first else ["o"])
    scale = {n: 1.0 for n in names}
    scale["q"] = float(np.float32(HD ** -0.5)) if first else float(np.float32(D ** -0.5)) / 2
    negate = -1.0 if first else -2.0

    ctx = ExitStack()
    with ctx:
        def sb(name, shape, dt=F32):
            return ctx.enter_context(nc.sbuf_tensor(f"{name}_{layer}", shape, dt))

        def psum(name, shape):
            return ctx.enter_context(nc.psum_tensor(f"{name}_{layer}", shape, F32))

        def sem(name):
            return ctx.enter_context(nc.semaphore(f"{name}_{layer}"))

        x_next = sb("x_next", [P, T, D])
        x_sb = sb("x", [P, T, D])
        bias = sb("bias", [P, 2, T, N])
        w_hi = {n: sb(f"w{n}_hi", [P, C, D], F32R) for n in names}
        w_lo = {n: sb(f"w{n}_lo", [P, C, D], F32R) for n in names}
        h = sb("h", [P, 2, D])
        ht_hi, ht_lo = (sb(f"ht_{s}", [P, C, N], F32R) for s in ("hi", "lo"))
        qk_parts = sb("qk_parts", [P, 4, N], F32R)
        qk_stack = sb("qk_stack", [SPLIT_ROWS, 2, 2, GH, N], F32R)
        v_stack = sb("v_stack", [P, T, PAIRS, 3, 2 * HD], F32R)
        masked = sb("masked", [P, 4, N])
        probs = sb("probs", [P, 4, N])
        pt_hi, pt_lo = (sb(f"pt_{s}", [P, 2, T, N], F32R) for s in ("hi", "lo"))
        out_t = sb("out_t", [P, N])
        neg_max = sb("neg_max", [P, 2, H, T])
        sums = sb("sums", [P, 2, H, T])
        rsum = sb("rsum", [P, 2, 2, T])
        stat = sb("stat", [P, T, 6])
        mean_var = sb("mean_var", [P, T, 2])
        var_eps, root0, sq, half_var, prod, fix, rstd, neg_mean, shift = (
            sb(n, [P, T]) for n in ("var_eps", "root0", "sq", "half_var", "prod", "fix", "rstd", "neg_mean", "shift"))
        eps, neg_half, one_half = (sb(n, [P, T]) for n in ("eps", "neg_half", "one_half"))
        ident = sb("ident", [P, P])
        fold = sb("fold", [P, 2 * HD])
        one_rows = sb("one_rows", [P, P], F32R)
        row_raw = sb("row_raw", [1, D])
        v_row = sb("v_row", [P, D], F32R)
        if first:
            qk_bias = sb("qk_bias", [P, 2, G])
            beta_col = sb("beta_col", [P, 1])
            scaled, hole = sb("scaled", [P, N]), sb("hole", [P, N])
            update = sb("update", [P, 2, T, 2 * HD])
        else:
            o_row = sb("o_row", [P, D], F32R)
            attn = sb("attn", [P, T, D])
            at_hi, at_lo = (sb(f"at_{s}", [P, T, C, P], F32R) for s in ("hi", "lo"))
            halves = sb("halves", [P, 2, T, N // 2])
            total = sb("total", [P, 2, H, T])
            size = sb("size", [P, 2, T])
            kept = sb("kept", [P, 2, 2, T])

        w_raw = {n: b[:].rearrange("p t n -> p (t n)")[:, 0:C * D].rearrange("p (c n) -> p c n", c=C)
                 for n, b in zip(names, (masked, probs, x_sb) if first else (masked, probs, x_sb, attn))}

        s_ps, t_ps, m_ps = (psum(n, [P, b, N]) for n, b in (("s_ps", 2), ("t_ps", 3), ("m_ps", 2)))
        o_ps = psum("o_ps", [P, N])

        w_loaded = {n: sem(f"w{n}_loaded") for n in names}
        w_upper, w_split = sem("w_upper"), sem("w_split")
        consts, consts_in = sem("consts"), sem("consts_in")
        next_loaded, x_loaded, x_stored = ([sem(f"{n}{t}") for t in range(T)]
                                           for n in ("next_loaded", "x_loaded", "x_stored"))
        adj_loaded = [sem(f"adj_loaded{s}") for s in range(2)]
        stacked = [[sem(f"stacked{s}{j}") for j in range(GH)] for s in range(2)]
        scores_done, masked_done, probs_done, turned = (
            sem(n) for n in ("scores_done", "masked_done", "probs_done", "turned"))
        hi_done, lo_done, weighed = (sem(n) for n in ("hi_done", "lo_done", "weighed"))
        out_copied, rsum_done = sem("out_copied"), sem("rsum_done")
        stat_done, mv_done, ln_steps, h_done = (sem(n) for n in ("stat_done", "mv_done", "ln_steps", "h_done"))
        made = {k: sem(f"{k}_made") for k in ("turn_h", "qk", "value", "turn_a", "project", "turn_out")}
        upper = {k: sem(f"{k}_upper") for k in ("turn_h", "qk", "value", "turn_a")}
        taken = {k: sem(f"{k}_taken") for k in ("turn_h", "qk", "value", "turn_a", "project", "turn_out")}
        per = {"turn_h": T, "qk": 2 * G, "value": T, "turn_a": T, "project": T, "turn_out": PAIRS}
        if first:
            bias_steps, bias_done, updated = sem("bias_steps"), sem("bias_done"), sem("updated")
        else:
            halved, folded, total_done, size_done, kept_done = (
                sem(n) for n in ("halved", "folded", "total_done", "size_done", "kept_done"))
        LN_STEPS = 9

        place = {(kind, k): n for n, (_, kind, k, _, _) in enumerate(side)}

        def bank_of(kind, k):
            return side[place[kind, k]][4]

        def bank_free(eng, kind, k, graph):
            job = graph.c - side[place[kind, k]][3]
            at = place[kind, k] - 1
            while at >= -2 * len(side):
                _, kind0, k0, off, bank = side[at % len(side)]
                before = Graph(job + off + at // len(side), graph.i)
                if bank == bank_of(kind, k) and before.exists():
                    wait(eng, taken[kind0], before.count(per[kind0], k0 + 1))
                    return
                at -= 1

        def tasks_at(step, graph, which):
            if step < 0:
                step, graph = step + STEPS, graph.prev()
            for steps, kind, k, off, _ in side:
                of = Graph(graph.c + off, graph.i)
                if of.exists() and (step in steps if which is None else step == steps[which]):
                    yield kind, k, of, steps

        def tile_of(step, graph, lag):
            n, g = step - lag, graph
            while n < 0:
                n, g = n + STEPS, g.prev()
            return (g, n) if n < STEPS and g.exists() else None

        def pair_of(step, graph, lag):
            at = tile_of(step, graph, lag)
            if at and at[1] % (2 * T) == T:
                return at[0], at[1] // (2 * T)
            return None

        def walk(eng, head, job):
            head(Graph(0))
            job(Graph(0), range(STEPS))
            with eng.Fori(0, (B - 2) // 2) as i:
                job(Graph(1, i), range(STEPS))
                job(Graph(2, i), range(STEPS))
            job(Graph(B - 1), range(STEPS))
            job(Graph(B), range(tail))

        block = ctx.enter_context(nc.Block())

        @block.sync
        def _(sp):
            def load_adj(g):
                wait(sp, masked_done, g.prev().count(STEPS, 0))
                sp.dma_start(bias[:, g.slot()], adj[g.number()].rearrange("(t p) n -> p t n", p=P)
                             ).then_inc(adj_loaded[g.slot()], 16)

            def load_next(g, t):
                wait(sp, h_done, g.prev().count(T, t + 1))
                sp.dma_start(x_next[:, t], x_in[g.number(), t * P:(t + 1) * P, :]).then_inc(next_loaded[t], 16)

            def load_x(g):
                for t in range(T):
                    wait(sp, x_stored[t], g.count(16, 0))
                    sp.dma_start(x_sb[:, t], x_in[g.number(), t * P:(t + 1) * P, :]).then_inc(x_loaded[t], 16)

            def store_x(g):
                for t in range(T):
                    if first:
                        wait(sp, updated, g.count(PAIRS, PAIRS))
                    else:
                        wait(sp, taken["project"], g.count(T, t + 1))
                    sp.dma_start(x_out[g.number(), t * P:(t + 1) * P, :], x_sb[:, t]).then_inc(x_stored[t], 16)

            def stack(g, grp):
                slot = g.group_slot(grp)
                wait(sp, taken["qk"], g.count(2 * G, 2 * grp + 2))
                for j in range(GH):
                    for r, pick in enumerate((slice(0, 3, 2), slice(0, 4, 3), slice(1, 3))):
                        sp.dma_start(qk_stack[r * HD:(r + 1) * HD, slot, :, j, :].bitcast(F32),
                                     qk_parts[j * HD:(j + 1) * HD, pick, :].bitcast(F32)
                                     ).then_inc(stacked[slot][j], 16)

            for t in range(T):
                load_next(Graph(0), t)
            for n, name in enumerate(names):
                sp.dma_start(w_raw[name], w_in[name].rearrange("(c p) n -> p c n", p=P)).then_inc(w_loaded[name], 16)
                if n == 0:
                    sp.dma_start(row_raw[:], b_in["v"].unsqueeze(0)).then_inc(consts_in, 16)
                    if first:
                        sp.dma_start(qk_bias[:, 0, :], b_in["q"].rearrange("(g p) -> p g", p=P),
                                     allow_slow_non_contiguous=True).then_inc(consts_in, 16)
                        sp.dma_start(qk_bias[:, 1, :], b_in["k"].rearrange("(g p) -> p g", p=P),
                                     allow_slow_non_contiguous=True).then_inc(consts_in, 16)
                        sp.dma_start(beta_col[:], beta.partition_broadcast(P)).then_inc(consts_in, 16)
            sp.dma_start(bias[:, 0], adj[0].rearrange("(t p) n -> p t n", p=P)).then_inc(adj_loaded[0], 16)
            if not first:
                sp.wait_ge(w_split, len(names) + 1)
                sp.dma_start(row_raw[:], b_in["o"].unsqueeze(0)).then_inc(consts_in, 16)

            def job(g, steps):
                if g.next().exists():
                    load_adj(g.next())
                    for t in range(T):
                        load_next(g.next(), t)
                if first and g.prev().exists():
                    store_x(g.prev())
                if g.exists():
                    stack(g, 1)
                    if first:
                        load_x(g)
                    stack(g, 2)
                if not first and g.prev().exists():
                    store_x(g.prev())
                if g.next().exists():
                    stack(g.next(), 0)
                if not first and g.exists():
                    load_x(g)

            walk(sp, lambda g: stack(g, 0), job)
            for t in range(T):
                sp.wait_ge(x_stored[t], 16 * B)

        @block.gpsimd
        def _(pool):
            nc.gpsimd.memset(ident[:], 0.0)
            nc.gpsimd.memset(fold[:], 0.0)
            nc.gpsimd.memset(one_rows[:].bitcast(F32), 0.0)
            nc.gpsimd.memset(v_row[:].bitcast(F32), 0.0)
            if not first:
                nc.gpsimd.memset(o_row[:].bitcast(F32), 0.0)
            nc.gpsimd.memset(eps[:], EPS)
            nc.gpsimd.memset(neg_half[:], -0.5)
            nc.gpsimd.memset(one_half[:], 1.5)
            nc.gpsimd.memset(v_stack[:].bitcast(F32), 0.0).then_inc(consts, 1)
            pool.wait_ge(consts, 1)
            nc.gpsimd.memset(one_rows[0:1, :].bitcast(F32), 1.0).then_inc(consts, 1)
            pool.wait_ge(consts, 2)
            nc.gpsimd.memset(one_rows[HD:HD + 1, :].bitcast(F32), 1.0).then_inc(consts, 1)
            pool.wait_ge(consts, 3)
            nc.gpsimd.affine_select(out=ident[:], in_=ident[:], compare_op=ALU.not_equal, fill=1.0, base=0,
                                    pattern=[[-1, P]], channel_multiplier=1).then_inc(consts, 1)
            for r in range(2):
                view = fold[:].rearrange("p (b c) -> p b c", b=2)
                nc.gpsimd.affine_select(out=view, in_=view, compare_op=ALU.not_equal, fill=1.0, base=-HD * r,
                                        pattern=[[-2 * HD, 2], [-1, HD]], channel_multiplier=1
                                        ).then_inc(consts, 1)
                pool.wait_ge(consts, 5 + r)

            def inverse_deviation(g):
                pool.wait_ge(mv_done, g.count(1, 1))
                wait(pool, h_done, g.count(T, 0))
                nc.gpsimd.tensor_tensor(var_eps[:], mean_var[:, :, 1], eps[:], ALU.add).then_inc(ln_steps, 1)
                pool.wait_ge(ln_steps, g.count(LN_STEPS, 1))
                nc.gpsimd.tensor_tensor(root0[:], var_eps[:], neg_half[:], ALU.pow).then_inc(ln_steps, 1)
                pool.wait_ge(ln_steps, g.count(LN_STEPS, 2))
                nc.gpsimd.tensor_tensor(sq[:], root0[:], root0[:], ALU.mult).then_inc(ln_steps, 1)
                nc.gpsimd.tensor_tensor(half_var[:], var_eps[:], neg_half[:], ALU.mult).then_inc(ln_steps, 1)
                nc.gpsimd.tensor_scalar(neg_mean[:], mean_var[:, :, 0], -1.0, None, ALU.mult).then_inc(ln_steps, 1)
                pool.wait_ge(ln_steps, g.count(LN_STEPS, 5))
                nc.gpsimd.tensor_tensor(prod[:], sq[:], half_var[:], ALU.mult).then_inc(ln_steps, 1)
                pool.wait_ge(ln_steps, g.count(LN_STEPS, 6))
                nc.gpsimd.tensor_tensor(fix[:], prod[:], one_half[:], ALU.add).then_inc(ln_steps, 1)
                pool.wait_ge(ln_steps, g.count(LN_STEPS, 7))
                nc.gpsimd.tensor_tensor(rstd[:], root0[:], fix[:], ALU.mult).then_inc(ln_steps, 1)
                pool.wait_ge(ln_steps, g.count(LN_STEPS, 8))
                nc.gpsimd.tensor_tensor(shift[:], neg_mean[:], rstd[:], ALU.mult).then_inc(ln_steps, 1)

            def make_bias(g, t):
                tile = bias[:, g.slot(), t, :]
                if t == 0:
                    pool.wait_ge(adj_loaded[g.slot()], g.slot_count(16))
                wait(pool, bias_done, g.count(T, t))
                nc.gpsimd.tensor_tensor(scaled[:], tile, beta_col[:].broadcast_to([P, N]), ALU.mult
                                        ).then_inc(bias_steps, 1)
                nc.gpsimd.tensor_scalar(hole[:], tile, 0.0, MASKED, ALU.is_le, ALU.mult).then_inc(bias_steps, 1)
                pool.wait_ge(bias_steps, g.count(2 * T, 2 * t + 2))
                nc.gpsimd.tensor_tensor(tile, scaled[:], hole[:], ALU.add).then_inc(bias_done, 1)

            def update_x(g, p):
                pool.wait_ge(taken["turn_out"], g.count(PAIRS, p + 1))
                if p == 0:
                    for t in range(T):
                        pool.wait_ge(x_loaded[t], g.count(16, 16))
                cols = x_sb[:, :, p * 2 * HD:(p + 1) * 2 * HD]
                nc.gpsimd.tensor_tensor(cols, cols, update[:, p % 2], ALU.add).then_inc(updated, 1)

            def total_of(g, n):
                u, t = n // T, n % T
                pool.wait_ge(masked_done, g.count(STEPS, n + 1))
                if t == 0:
                    wait(pool, total_done, g.count(H, u - 1))
                nc.gpsimd.tensor_tensor(halves[:, u % 2, t, :], masked[:, n % 4, 0:N // 2],
                                        masked[:, n % 4, N // 2:N], ALU.add).then_inc(halved, 1)
                if t == T - 1:
                    pool.wait_ge(halved, g.count(STEPS, n + 1))
                    for level, w in enumerate((N // 4, N // 8, N // 16)):
                        nc.gpsimd.tensor_tensor(halves[:, u % 2, :, 0:w], halves[:, u % 2, :, 0:w],
                                                halves[:, u % 2, :, w:2 * w], ALU.add).then_inc(folded, 1)
                        pool.wait_ge(folded, g.count(3 * H, 3 * u + level + 1))

            def head(g):
                if first:
                    pool.wait_ge(consts_in, 16 * 4)
                    for t in range(T):
                        make_bias(g, t)
                inverse_deviation(g)

            def job(g, steps):
                for step in steps:
                    if not first and g.exists():
                        total_of(g, step)
                    if first and g.next().exists() and step in BIAS_STEPS:
                        make_bias(g.next(), BIAS_STEPS.index(step))
                    if step == moments_step + 1 and g.exists() and g.next().exists():
                        inverse_deviation(g.next())
                    at = pair_of(step, g, LAG_NORM)
                    if first and at:
                        update_x(*at)

            walk(pool, head, job)

        @block.scalar
        def _(act):
            def apply_norm(g, t):
                if t == 0:
                    act.wait_ge(ln_steps, g.count(LN_STEPS, LN_STEPS))
                wait(act, made["turn_h"], g.count(T, max(t - 1, 0)))
                nc.scalar.activation(h[:, t % 2, :], x_next[:, t, :], ACT.Relu, bias=shift[:, t:t + 1],
                                     scale=rstd[:, t:t + 1]).then_inc(h_done, 1)

            def upper_part(kind, k, g, bank):
                act.wait_ge(made[kind], g.count(per[kind], k + 1))
                if kind == "turn_h":
                    nc.scalar.activation(ht_hi[:, :, k * P:(k + 1) * P],
                                         m_ps[:, bank, 0:D].rearrange("p (c n) -> p c n", c=C),
                                         ACT.Copy).then_inc(upper[kind], 1)
                elif kind == "turn_a":
                    nc.scalar.activation(at_hi[:, k], m_ps[:, bank, 0:D].rearrange("p (c n) -> p c n", c=C),
                                         ACT.Copy).then_inc(upper[kind], 1)
                elif kind == "value":
                    nc.scalar.activation(v_stack[:, k, :, 0:3:2, 0:HD],
                                         m_ps[:, bank, 0:D].rearrange("p (a b d) -> p a b d", b=2, d=HD),
                                         ACT.Copy).then_inc(upper[kind], 1)
                elif kind == "qk":
                    grp, which = k // 2, k % 2
                    if which == 0 and not (g.i is None and g.c == 0 and grp == 0):
                        for j in range(GH):
                            act.wait_ge(stacked[1 - g.group_slot(grp)][j], g.group_count(grp, 16 * STACKS, 1))
                    if first:
                        nc.scalar.activation(qk_parts[:, 2 * which, :], m_ps[:, bank, :], ACT.Identity,
                                             bias=qk_bias[:, which, grp:grp + 1]).then_inc(upper[kind], 1)
                    else:
                        nc.scalar.activation(qk_parts[:, 2 * which, :], m_ps[:, bank, :], ACT.Copy).then_inc(upper[kind], 1)

            for name in names:
                act.wait_ge(w_loaded[name], 16)
                nc.scalar.activation(w_hi[name][:], w_raw[name], ACT.Copy, scale=scale[name]).then_inc(w_upper, 1)
            act.wait_ge(consts_in, 16 * (4 if first else 1))
            act.wait_ge(consts, 1)
            nc.scalar.activation(v_row[0:1, :], row_raw[:], ACT.Copy).then_inc(w_upper, 1)
            if not first:
                act.wait_ge(consts_in, 32)
                nc.scalar.activation(o_row[0:1, :], row_raw[:], ACT.Copy).then_inc(w_upper, 1)

            def head(g):
                for t in range(T):
                    apply_norm(g, t)
                    upper_part("turn_h", t, g, bank_of("turn_h", t))
                for k in range(2):
                    upper_part("qk", k, g, bank_of("qk", k))

            def job(g, steps):
                for step in steps:
                    for kind, k, of, _ in tasks_at(step - 1, g, -1):
                        if kind in upper:
                            upper_part(kind, k, of, bank_of(kind, k))
                    for kind, k, of, _ in tasks_at(step + 1, g, 0):
                        if kind == "turn_h":
                            apply_norm(of, k)
                    at = pair_of(step, g, LAG_COPY)
                    if at:
                        act.wait_ge(weighed, at[0].count(STEPS, (2 * at[1] + 2) * T))
                        wait(act, made["turn_out"], at[0].count(PAIRS, at[1]))
                        nc.scalar.activation(out_t[:], o_ps[:], ACT.Copy).then_inc(out_copied, 1)
                    at = tile_of(step, g, LAG_TURN)
                    if at:
                        of, n = at
                        u, t = n // T, n % T
                        act.wait_ge(turned, of.count(STEPS, n + 1))
                        if t == 0:
                            wait(act, weighed, of.count(STEPS, (u - 1) * T))
                        nc.scalar.activation(pt_hi[:, u % 2, :, t * P:(t + 1) * P],
                                             t_ps[:, n % 3, :].rearrange("p (c q) -> p c q", c=T),
                                             ACT.Copy).then_inc(hi_done, 1)
                    if g.exists():
                        n = step
                        u, t = n // T, n % T
                        act.wait_ge(masked_done, g.count(STEPS, n + 1))
                        wait(act, turned, g.count(STEPS, n - 3))
                        if n == 0 and g.prev().exists():
                            act.wait_ge(rsum_done, g.prev().count(PAIRS, 1))
                        nc.scalar.activation(probs[:, n % 4, :], masked[:, n % 4, :], ACT.Exp,
                                             bias=neg_max[:, g.slot(), u, t:t + 1], scale=-1.0,
                                             accum_out=sums[:, g.slot(), u, t:t + 1]).then_inc(probs_done, 1)

            walk(act, head, job)

        @block.vector
        def _(dve):
            def lower_part(kind, k, g, bank):
                if kind == "project":
                    dve.wait_ge(made[kind], g.count(T, k + 1))
                    dve.wait_ge(x_loaded[k], g.count(16, 16))
                    row = x_sb[:, k, :]
                    nc.vector.tensor_tensor(row, m_ps[:, bank, 0:D], row, ALU.add).then_inc(taken[kind], 1)
                    return
                dve.wait_ge(upper[kind], g.count(per[kind], k + 1))
                if kind == "turn_h":
                    cols = slice(k * P, (k + 1) * P)
                    nc.vector.tensor_tensor(ht_lo[:, :, cols], m_ps[:, bank, 0:D].rearrange("p (c n) -> p c n", c=C),
                                            ht_hi[:, :, cols].bitcast(F32), ALU.subtract).then_inc(taken[kind], 1)
                elif kind == "turn_a":
                    nc.vector.tensor_tensor(at_lo[:, k], m_ps[:, bank, 0:D].rearrange("p (c n) -> p c n", c=C),
                                            at_hi[:, k].bitcast(F32), ALU.subtract).then_inc(taken[kind], 1)
                elif kind == "value":
                    nc.vector.tensor_tensor(v_stack[:, k, :, 0:3:2, HD:2 * HD],
                                            m_ps[:, bank, 0:D].rearrange("p (a b d) -> p a b d", b=2, d=HD),
                                            v_stack[:, k, :, 0:3:2, 0:HD].bitcast(F32), ALU.subtract
                                            ).then_inc(taken[kind], 1)
                elif kind == "qk":
                    grp, which = k // 2, k % 2
                    if first:
                        nc.vector.scalar_tensor_tensor(out=qk_parts[:, 2 * which + 1, :], in0=m_ps[:, bank, :],
                                                       scalar=qk_bias[:, which, grp:grp + 1],
                                                       in1=qk_parts[:, 2 * which, :].bitcast(F32), op0=ALU.add,
                                                       op1=ALU.subtract).then_inc(taken[kind], 1)
                    else:
                        nc.vector.tensor_tensor(qk_parts[:, 2 * which + 1, :], m_ps[:, bank, :],
                                                qk_parts[:, 2 * which, :].bitcast(F32), ALU.subtract
                                                ).then_inc(taken[kind], 1)

            def statistics(g, t):
                dve.wait_ge(next_loaded[t], g.count(16, 16))
                nc.vector.bn_stats(stat[:, t, :], x_next[:, t, :]).then_inc(stat_done, 1)

            def moments_wait(g):
                dve.wait_ge(stat_done, g.count(T, T))
                wait(dve, ln_steps, g.count(LN_STEPS, 0))

            def moments():
                for t in range(T):
                    last = nc.vector.bn_aggr(mean_var[:, t, :], stat[:, t, :])
                last.then_inc(mv_done, 1)

            for n, name in enumerate(names):
                dve.wait_ge(w_upper, n + 1)
                nc.vector.scalar_tensor_tensor(out=w_lo[name][:].rearrange("p c n -> p (c n)"),
                                               in0=w_raw[name].rearrange("p c n -> p (c n)"), scalar=scale[name],
                                               in1=w_hi[name][:].rearrange("p c n -> p (c n)").bitcast(F32),
                                               op0=ALU.mult, op1=ALU.subtract).then_inc(w_split, 1)
            if first:
                nc.vector.tensor_scalar(qk_bias[:, 0, :], qk_bias[:, 0, :], scale["q"], None, ALU.mult
                                        ).then_inc(w_split, 1)
            dve.wait_ge(w_upper, len(names) + 1)
            nc.vector.tensor_tensor(v_row[HD:HD + 1, :], row_raw[:], v_row[0:1, :].bitcast(F32), ALU.subtract
                                    ).then_inc(w_split, 1)
            if not first:
                dve.wait_ge(w_upper, len(names) + 2)
                nc.vector.tensor_tensor(o_row[HD:HD + 1, :], row_raw[:], o_row[0:1, :].bitcast(F32),
                                        ALU.subtract).then_inc(w_split, 1)

            def head(g):
                for t in range(T):
                    statistics(g, t)
                moments_wait(g)
                moments()
                for t in range(T):
                    lower_part("turn_h", t, g, bank_of("turn_h", t))
                for k in range(2):
                    lower_part("qk", k, g, bank_of("qk", k))
                if first:
                    dve.wait_ge(bias_done, T)
                else:
                    dve.wait_ge(adj_loaded[0], 16)

            def out_rows(g, p, stage):
                sl = g.slot()
                mine = slice(2 * p, 2 * p + 2)
                if stage == 0:
                    dve.wait_ge(probs_done, g.count(STEPS, (2 * p + 2) * T))
                    wait(dve, taken["turn_out"], g.count(PAIRS, p - 1))
                    nc.vector.reciprocal(rsum[:, p % 2], sums[:, sl, mine, :]).then_inc(rsum_done, 1)
                    if not first:
                        dve.wait_ge(total_done, g.count(H, 2 * p + 2))
                        wait(dve, kept_done, g.count(PAIRS, p))
                        nc.vector.scalar_tensor_tensor(
                            out=size[:].rearrange("p h t -> p (h t)"),
                            in0=neg_max[:, sl, mine, :].rearrange("p h t -> p (h t)"), scalar=0.0,
                            in1=total[:, sl, mine, :].rearrange("p h t -> p (h t)"), op0=ALU.not_equal, op1=ALU.max
                        ).then_inc(size_done, 1)
                elif stage == 1 and not first:
                    dve.wait_ge(size_done, g.count(PAIRS, p + 1))
                    dve.wait_ge(rsum_done, g.count(PAIRS, p + 1))
                    nc.vector.scalar_tensor_tensor(
                        out=kept[:, p % 2].rearrange("p h t -> p (h t)"), in0=size[:].rearrange("p h t -> p (h t)"),
                        scalar=0.0, in1=rsum[:, p % 2].rearrange("p h t -> p (h t)"), op0=ALU.is_gt, op1=ALU.mult
                    ).then_inc(kept_done, 1)
                elif stage == 2:
                    dve.wait_ge(made["turn_out"], g.count(PAIRS, p + 1))
                    factor = rsum if first else kept
                    if first:
                        dve.wait_ge(rsum_done, g.count(PAIRS, p + 1))
                        wait(dve, updated, g.count(PAIRS, p - 1))
                        out = update[:, p % 2].rearrange("p t (h d) -> p t h d", h=2)
                    else:
                        dve.wait_ge(kept_done, g.count(PAIRS, p + 1))
                        if p == 0:
                            wait(dve, made["turn_a"], g.count(T, 0))
                        out = attn[:, :, p * 2 * HD:(p + 1) * 2 * HD].rearrange("p t (h d) -> p t h d", h=2)
                    by = factor[:, p % 2].rearrange("p h t -> p t h").unsqueeze(3).broadcast_to([P, T, 2, HD])
                    nc.vector.tensor_tensor(out, m_ps[:, bank_of("turn_out", p), 0:N // 2].rearrange("p (t h d) -> p t h d", t=T, h=2), by,
                                            ALU.mult).then_inc(taken["turn_out"], 1)

            def job(g, steps):
                for step in steps:
                    for kind, k, of, _ in tasks_at(step - 2, g, -1):
                        if kind != "turn_out":
                            lower_part(kind, k, of, bank_of(kind, k))
                    if g.exists() and g.next().exists():
                        if step in stats_steps:
                            statistics(g.next(), stats_steps.index(step))
                        if step == moments_step:
                            moments_wait(g.next())
                    for stage, lag in enumerate((LAG_COPY, LAG_OUT, LAG_NORM)):
                        at = pair_of(step, g, lag)
                        if at:
                            out_rows(*at, stage)
                    if not first:
                        at = tile_of(step, g, LAG_TOTAL)
                        if at and at[1] % T == 0:
                            of, u = at[0], at[1] // T
                            dve.wait_ge(folded, of.count(3 * H, 3 * u + 3))
                            nc.vector.tensor_reduce(total[:, of.slot(), u, :], halves[:, u % 2, :, 0:N // 16], AX.X,
                                                    ALU.add).then_inc(total_done, 1)
                    if g.exists():
                        n = step
                        dve.wait_ge(scores_done, g.count(STEPS, n + 1))
                        if n == 0 and not (g.i is None and g.c == 0):
                            if first:
                                dve.wait_ge(bias_done, g.count(T, T))
                            else:
                                dve.wait_ge(adj_loaded[g.slot()], g.slot_count(16))
                        wait(dve, probs_done, g.count(STEPS, n - 3))
                        if not first:
                            wait(dve, halved, g.count(STEPS, n - 3))
                    at = tile_of(step, g, LAG_LO)
                    if at:
                        of, n = at
                        u, t = n // T, n % T
                        dve.wait_ge(hi_done, of.count(STEPS, n + 1))
                        dst = (slice(None), u % 2, slice(None), slice(t * P, (t + 1) * P))
                        nc.vector.tensor_tensor(pt_lo[dst], t_ps[:, n % 3, :].rearrange("p (c q) -> p c q", c=T),
                                                pt_hi[dst].bitcast(F32), ALU.subtract).then_inc(lo_done, 1)
                    if g.exists():
                        n = step
                        u, t = n // T, n % T
                        nc.vector.tensor_tensor_reduce(
                            out=masked[:, n % 4, :], in0=s_ps[:, n % 2, :], in1=bias[:, g.slot(), t, :], scale=negate,
                            scalar=BIG, op0=ALU.add, op1=ALU.min, accum_out=neg_max[:, g.slot(), u, t:t + 1]
                        ).then_inc(masked_done, 1)
                        if step == moments_step and g.next().exists():
                            moments()

            walk(dve, head, job)

        @block.tensor
        def _(pe):
            def three_passes(out, a_hi, a_lo, b_hi, b_lo, row, part, parts):
                terms = [(a[c], b[c]) for c in range(C) for a, b in ((a_hi, b_hi), (a_hi, b_lo), (a_lo, b_hi))]
                if row is not None:
                    terms.append((one_rows[:], row[:]))
                for n in range(len(terms) * part // parts, len(terms) * (part + 1) // parts):
                    last = nc.tensor.matmul(out, *terms[n], start=n == 0, stop=n == len(terms) - 1)
                return last

            def make(kind, k, g, part=0, parts=1):
                out = m_ps[:, bank_of(kind, k), :]
                if part == 0:
                    bank_free(pe, kind, k, g)
                if kind == "turn_h":
                    pe.wait_ge(h_done, g.count(T, k + 1))
                    for c in range(C):
                        last = nc.tensor.transpose(out[:, c * P:(c + 1) * P], h[:, k % 2, c * P:(c + 1) * P], ident[:])
                elif kind == "turn_a":
                    pe.wait_ge(taken["turn_out"], g.count(PAIRS, PAIRS))
                    for c in range(C):
                        last = nc.tensor.transpose(out[:, c * P:(c + 1) * P], attn[:, k, c * P:(c + 1) * P], ident[:])
                elif kind == "project":
                    if part == 0:
                        pe.wait_ge(taken["turn_a"], g.count(T, k + 1))
                    last = three_passes(out[:, 0:D], *([x[:, k, c, :] for c in range(C)] for x in (at_hi, at_lo)),
                                        *([w["o"][:, c, :] for c in range(C)] for w in (w_hi, w_lo)), o_row, part, parts)
                elif kind == "value":
                    pe.wait_ge(taken["turn_h"], g.count(T, T))
                    rows = slice(k * P, (k + 1) * P)
                    last = three_passes(out[:, 0:D], *([x[:, c, rows] for c in range(C)] for x in (ht_hi, ht_lo)),
                                        *([w["v"][:, c, :] for c in range(C)] for w in (w_hi, w_lo)), v_row, part, parts)
                elif kind == "qk":
                    if part == 0:
                        pe.wait_ge(taken["turn_h"], g.count(T, T))
                    name, cols = "qk"[k % 2], slice(k // 2 * P, (k // 2 + 1) * P)
                    last = three_passes(out, *([w[name][:, c, cols] for c in range(C)] for w in (w_hi, w_lo)),
                                        *([x[:, c, :] for c in range(C)] for x in (ht_hi, ht_lo)), None, part, parts)
                elif kind == "turn_out":
                    pe.wait_ge(out_copied, g.count(PAIRS, k + 1))
                    for t in range(T):
                        last = nc.tensor.matmul(out[:, t * 2 * HD:(t + 1) * 2 * HD], out_t[:, t * P:(t + 1) * P],
                                                fold[:], start=True, stop=True)
                if part == parts - 1:
                    last.then_inc(made[kind], 1)

            def weigh(g, u, c):
                if c == 0:
                    pe.wait_ge(lo_done, g.count(STEPS, (u + 1) * T))
                    if u % 2 == 0:
                        wait(pe, out_copied, g.count(PAIRS, u // 2))
                if u == 0:
                    pe.wait_ge(taken["value"], g.count(T, c + 1))
                values = v_stack[:, c, u // 2].rearrange("p a b -> p (a b)")
                values = values[:, 0:P] if u % 2 == 0 else values[:, 2 * HD:2 * HD + P]
                nc.tensor.matmul(o_ps[:], values, pt_hi[:, u % 2, c, :], start=u % 2 == 0 and c == 0, stop=False)
                nc.tensor.matmul(o_ps[:], values, pt_lo[:, u % 2, c, :], start=False,
                                 stop=u % 2 == 1 and c == T - 1).then_inc(weighed, 1)

            pe.wait_ge(consts, 6)
            pe.wait_ge(w_split, len(names) + 2)

            def head(g):
                for t in range(T):
                    make("turn_h", t, g)
                for k in range(2):
                    make("qk", k, g)

            def job(g, steps):
                for step in steps:
                    if g.exists():
                        n = step
                        u, t = n // T, n % T
                        grp, j = u // GH, u % GH
                        slot = g.group_slot(grp)
                        if t == 0:
                            pe.wait_ge(stacked[slot][j], g.group_count(grp, 16 * STACKS))
                        wait(pe, masked_done, g.count(STEPS, n - 1))
                        nc.tensor.matmul(s_ps[:, n % 2, :], qk_stack[:, slot, 0, j, t * P:(t + 1) * P],
                                         qk_stack[:, slot, 1, j, :], start=True, stop=True).then_inc(scores_done, 1)
                    for lag in range(LAG_WEIGH[0][-1], LAG_WEIGH[1][0] - 1, -1):
                        at = tile_of(step, g, lag)
                        if at and at[1] % T == 0:
                            u = at[1] // T
                            for c in range(T):
                                if LAG_WEIGH[u % 2][c] == lag:
                                    weigh(at[0], u, c)
                    at = tile_of(step, g, LAG_TURN)
                    if at:
                        of, n = at
                        pe.wait_ge(probs_done, of.count(STEPS, n + 1))
                        wait(pe, lo_done, of.count(STEPS, n - 2))
                        for c in range(T):
                            last = nc.tensor.transpose(t_ps[:, n % 3, c * P:(c + 1) * P],
                                                       probs[:, n % 4, c * P:(c + 1) * P], ident[:])
                        last.then_inc(turned, 1)
                    for kind, k, of, parts in tasks_at(step, g, None):
                        make(kind, k, of, parts.index(step), len(parts))

            walk(pe, head, job)


def graph_attention_kernel(nc, x, adj, q0, bq0, k0, bk0, v0, bv0, beta, q1, k1, v1, bv1, o1, bo1, out):
    between = nc.dram_tensor("between_dram", (B, N, D), F32, kind="Internal").ap()
    layer_pass(nc, 0, x, adj, {"q": q0, "k": k0, "v": v0}, {"q": bq0, "k": bk0, "v": bv0}, beta, between)
    layer_pass(nc, 1, between, adj, {"q": q1, "k": k1, "v": v1, "o": o1}, {"v": bv1, "o": bo1}, None, out)


def kernel(**inputs):
    import numpy as _np
    import concourse.bacc as _bacc
    from concourse import mybir as _mybir
    from concourse.bass_utils import run_bass_kernel_spmd as _run

    nc = _bacc.Bacc("TRN2", target_bir_lowering=False, num_devices=1, dynamic_dma_scratch_size=1024)
    names = ["x", "adj", "L0_gnn_Wq", "L0_gnn_bq", "L0_gnn_Wk", "L0_gnn_bk", "L0_gnn_Wv", "L0_gnn_bv",
             "L0_gnn_beta", "L1_gnn_Wq", "L1_gnn_Wk", "L1_gnn_Wv", "L1_gnn_bv", "L1_gnn_Wo", "L1_gnn_bo"]
    transposed = {"L1_gnn_Wq", "L1_gnn_Wk", "L1_gnn_Wv", "L1_gnn_Wo"}
    arrays, args = {}, []
    for name in names:
        a = _np.asarray(inputs[name])
        a = a.T if name in transposed else a
        a = _np.ascontiguousarray(a.reshape(1) if a.ndim == 0 else a)
        arrays[f"in_{name}_dram"] = a
        args.append(nc.dram_tensor(f"in_{name}_dram", a.shape, _mybir.dt.from_np(a.dtype), kind="ExternalInput").ap())
    out = nc.dram_tensor("out_dram", (16, 512, 384), _mybir.dt.float32, kind="ExternalOutput").ap()
    graph_attention_kernel(nc, *args, out)
    r = _run(nc, [arrays], core_ids=[0])
    return r.results[0]["out_dram"]
```

```python
from contextlib import ExitStack

import concourse.bass as bass
from concourse import mybir
import numpy as np

F32 = mybir.dt.float32
F32R = mybir.dt.float32r
ALU = mybir.AluOpType
ACT = mybir.ActivationFunctionType
AX = mybir.AxisListType

B, N, D, H = 16, 512, 384, 12
HD = D // H
P = 128
T = N // P
C = D // P
GH = P // HD
G = H // GH
STEPS = H * T
PAIRS = H // 2
EPS = 1e-5
MASKED = -9000000000000000.0
BIG = 3.0e38
SPLIT_ROWS = 3 * HD
STACKS = 3

BIAS_STEPS = (4, 20, 28, 36)
ROW_BIAS_STEPS = ((14, 15, 16, 17), (13, 17, 21, 29))
LAG_TURN = 2
LAG_LO = 3
LAG_TOTAL = T + 3
LAG_WEIGH = ((8, 8, 9, 10), (7, 8, 9, 10))
LAG_COPY, LAG_OUT, LAG_NORM = T + 7, T + 9, T + 11


class Graph:

    def __init__(self, c, i=None):
        self.c, self.i = c, i

    def next(self):
        return Graph(self.c + 1, self.i)

    def prev(self):
        return Graph(self.c - 1, self.i)

    def exists(self):
        return self.i is not None or 0 <= self.c < B

    def slot(self):
        return self.c % 2

    def number(self):
        return self.c if self.i is None else self.i * 2 + self.c

    def count(self, per_graph, more):
        c = self.c * per_graph + more
        assert self.i is None or c > 0, "a wait on zero"
        return c if self.i is None else self.i * (2 * per_graph) + c

    def slot_count(self, by):
        c = by * (self.c // 2 + 1)
        return c if self.i is None else self.i * by + c

    def group_slot(self, g):
        return (G * self.c + g) % 2

    def group_count(self, g, by, back=0):
        c = by * ((G * self.c + g - back) // 2 + 1)
        return c if self.i is None else self.i * (G * by) + c


def wait(eng, sem, value):
    if not isinstance(value, int) or value > 0:
        eng.wait_ge(sem, value)


def side_tasks(layer):
    tasks = []

    def add(kind, k, off, bank, first, parts):
        steps = tuple(first + n for n, count in enumerate(parts) for _ in range(count))
        tasks.append((steps, kind, k, off, bank))

    for p, bank in enumerate((1, 0, 1, 1, 1, 0) if layer else (1, 1, 0, 1, 0, 0)):
        step = 2 * T * p + T + LAG_OUT
        add("turn_out", p, -(step // STEPS), bank, step % STEPS, (1, 1))
    if layer == 0:
        add("qk", 3, 0, 1, 0, (2, 1, 2, 4))
        add("value", 0, 0, 0, 3, (1, 8))
        add("value", 1, 0, 1, 5, (9,))
        add("value", 2, 0, 0, 5, (1, 8))
        add("value", 3, 0, 1, 7, (9,))
        add("qk", 4, 0, 1, 12, (3, 3, 2, 1))
        add("qk", 5, 0, 0, 14, (3, 3, 2, 1))
        add("turn_h", 0, 1, 0, 19, (1,))
        add("turn_h", 1, 1, 1, 21, (1,))
        add("turn_h", 2, 1, 0, 23, (1,))
        add("turn_h", 3, 1, 0, 26, (1,))
        add("qk", 0, 1, 0, 28, (1, 2, 3, 3))
        add("qk", 1, 1, 1, 31, (1, 0, 1, 0, 2, 1, 2, 1, 1))
        add("qk", 2, 1, 0, 36, (2, 0, 0, 2, 0, 0, 0, 1, 0, 0, 2, 2))
    else:
        add("qk", 2, 0, 0, 0, (2, 2, 3, 2))
        add("value", 0, 0, 1, 4, (10,))
        add("value", 1, 0, 0, 5, (10,))
        add("value", 2, 0, 1, 6, (10,))
        add("value", 3, 0, 0, 7, (10,))
        add("qk", 3, 0, 1, 9, (3, 2, 4))
        add("turn_a", 0, -1, 0, 12, (1,))
        add("turn_a", 1, -1, 1, 13, (1,))
        add("turn_a", 2, -1, 0, 14, (1,))
        add("turn_a", 3, -1, 1, 15, (1,))
        add("qk", 4, 0, 0, 16, (3, 1, 0, 4, 1))
        add("qk", 5, 0, 1, 20, (2, 3, 4))
        add("turn_h", 0, 1, 0, 23, (1,))
        add("turn_h", 1, 1, 1, 24, (1,))
        add("turn_h", 2, 1, 1, 26, (1,))
        add("turn_h", 3, 1, 0, 28, (1,))
        add("project", 0, -1, 1, 28, (4, 4, 1))
        add("qk", 0, 1, 0, 30, (2, 0, 1, 1, 1, 4))
        add("qk", 1, 1, 1, 35, (3, 3, 1, 2))
        add("project", 1, -1, 0, 38, (2, 5, 2))
        add("project", 2, -1, 0, 42, (1, 1, 2, 2, 3))
        add("project", 3, -1, 1, 45, (4, 4, 1))
    tasks.sort()
    for bank in range(2):
        mine = [steps for steps, _, _, _, b in tasks if b == bank]
        assert all(one[-1] < other[0] for one, other in zip(mine, mine[1:]))
    return tasks


def layer_pass(nc, layer, x_in, adj, w_in, b_in, beta, x_out):
    first = layer == 0
    side = side_tasks(layer)
    ahead = sum(kind == "qk" and off == 1 for _, kind, _, off, _ in side)
    stats_steps = (4, 5, 6, 7)
    moments_step = stats_steps[-1] + 1
    tail = max(LAG_NORM, *(steps[-1] + 2 for steps, _, _, off, _ in side if off < 0)) + 1
    names = ["q", "k", "v"] + ([] if first else ["o"])
    scale = {n: 1.0 for n in names}
    scale["q"] = float(np.float32(HD ** -0.5)) if first else float(np.float32(D ** -0.5)) / 2
    negate = -1.0 if first else -2.0
    CONSTS = 4 if first else 6
    CONSTS_IN = 4 if first else 2

    ctx = ExitStack()
    with ctx:
        def sb(name, shape, dt=F32):
            return ctx.enter_context(nc.sbuf_tensor(f"{name}_{layer}", shape, dt))

        def psum(name, shape):
            return ctx.enter_context(nc.psum_tensor(f"{name}_{layer}", shape, F32))

        def sem(name):
            return ctx.enter_context(nc.semaphore(f"{name}_{layer}"))

        x_next = sb("x_next", [P, T, D])
        x_sb = sb("x", [P, T, D])
        bias = sb("bias", [P, 2, T, N])
        w_hi = {n: sb(f"w{n}_hi", [P, C, D], F32R) for n in names}
        w_lo = {n: sb(f"w{n}_lo", [P, C, D], F32R) for n in names}
        h = sb("h", [P, 2, D])
        ht_hi, ht_lo = (sb(f"ht_{s}", [P, C, N], F32R) for s in ("hi", "lo"))
        qk_parts = sb("qk_parts", [P, 4, N], F32R)
        qk_stack = sb("qk_stack", [SPLIT_ROWS, 2, 2, GH, N], F32R)
        v_stack = sb("v_stack", [P, T, PAIRS, 3, 2 * HD], F32R)
        masked = sb("masked", [P, 4, N])
        probs = sb("probs", [P, 4, N])
        pt_hi, pt_lo = (sb(f"pt_{s}", [P, 2, T, N], F32R) for s in ("hi", "lo"))
        out_t = sb("out_t", [P, N])
        neg_max = sb("neg_max", [P, 2, H, T])
        sums = sb("sums", [P, 2, H, T])
        rsum = sb("rsum", [P, 2, 2, T])
        stat = sb("stat", [P, T, 6])
        mean_var = sb("mean_var", [P, T, 2])
        var_eps, root0, sq, half_var, prod, fix, rstd, neg_mean, shift = (
            sb(n, [P, T]) for n in ("var_eps", "root0", "sq", "half_var", "prod", "fix", "rstd", "neg_mean", "shift"))
        eps, neg_half, one_half = (sb(n, [P, T]) for n in ("eps", "neg_half", "one_half"))
        ident = sb("ident", [P, P])
        fold = sb("fold", [P, 2 * HD])
        row_bias = sb("row_bias", [P, D])
        if first:
            qk_bias = sb("qk_bias", [P, 2, G])
            beta_col = sb("beta_col", [P, 1])
            scaled, hole = sb("scaled", [P, N]), sb("hole", [P, N])
            update = sb("update", [P, 2, T, 2 * HD])
        else:
            one_rows = sb("one_rows", [P, P], F32R)
            row_raw = sb("row_raw", [1, D])
            v_row = sb("v_row", [P, D], F32R)
            attn = sb("attn", [P, T, D])
            at_hi, at_lo = (sb(f"at_{s}", [P, T, C, P], F32R) for s in ("hi", "lo"))
            halves = sb("halves", [P, 2, T, N // 2])
            total = sb("total", [P, 2, H, T])
            size = sb("size", [P, 2, T])
            kept = sb("kept", [P, 2, 2, T])

        w_raw = {n: b[:].rearrange("p t n -> p (t n)")[:, 0:C * D].rearrange("p (c n) -> p c n", c=C)
                 for n, b in zip(names, (masked, probs, x_sb) if first else (masked, probs, x_sb, attn))}

        s_ps, t_ps, m_ps = (psum(n, [P, b, N]) for n, b in (("s_ps", 2), ("t_ps", 3), ("m_ps", 2)))
        o_ps = psum("o_ps", [P, N])

        w_loaded = {n: sem(f"w{n}_loaded") for n in names}
        w_upper, w_split = sem("w_upper"), sem("w_split")
        consts, consts_in, biased = sem("consts"), sem("consts_in"), sem("biased")
        next_loaded, x_loaded, x_stored = ([sem(f"{n}{t}") for t in range(T)]
                                           for n in ("next_loaded", "x_loaded", "x_stored"))
        adj_loaded = [sem(f"adj_loaded{s}") for s in range(2)]
        stacked = [[sem(f"stacked{s}{j}") for j in range(GH)] for s in range(2)]
        scores_done, masked_done, probs_done, turned = (
            sem(n) for n in ("scores_done", "masked_done", "probs_done", "turned"))
        hi_done, lo_done, weighed = (sem(n) for n in ("hi_done", "lo_done", "weighed"))
        out_copied, rsum_done = sem("out_copied"), sem("rsum_done")
        stat_done, mv_done, ln_steps, h_done = (sem(n) for n in ("stat_done", "mv_done", "ln_steps", "h_done"))
        made = {k: sem(f"{k}_made") for k in ("turn_h", "qk", "value", "turn_a", "project", "turn_out")}
        upper = {k: sem(f"{k}_upper") for k in ("turn_h", "qk", "value", "turn_a")}
        taken = {k: sem(f"{k}_taken") for k in ("turn_h", "qk", "value", "turn_a", "project", "turn_out")}
        per = {"turn_h": T, "qk": 2 * G, "value": T, "turn_a": T, "project": T, "turn_out": PAIRS}
        if first:
            bias_steps, bias_done, updated = sem("bias_steps"), sem("bias_done"), sem("updated")
        else:
            halved, folded, total_done, size_done, kept_done = (
                sem(n) for n in ("halved", "folded", "total_done", "size_done", "kept_done"))
        LN_STEPS = 9

        place = {(kind, k): n for n, (_, kind, k, _, _) in enumerate(side)}

        def bank_of(kind, k):
            return side[place[kind, k]][4]

        def bank_free(eng, kind, k, graph):
            job = graph.c - side[place[kind, k]][3]
            at = place[kind, k] - 1
            while at >= -2 * len(side):
                _, kind0, k0, off, bank = side[at % len(side)]
                before = Graph(job + off + at // len(side), graph.i)
                if bank == bank_of(kind, k) and before.exists():
                    wait(eng, taken[kind0], before.count(per[kind0], k0 + 1))
                    return
                at -= 1

        def tasks_at(step, graph, which):
            if step < 0:
                step, graph = step + STEPS, graph.prev()
                if not graph.exists():
                    return
            for steps, kind, k, off, _ in side:
                of = Graph(graph.c + off, graph.i)
                if of.exists() and (step in steps if which is None else step == steps[which]):
                    yield kind, k, of, steps

        def tile_of(step, graph, lag):
            n, g = step - lag, graph
            while n < 0:
                n, g = n + STEPS, g.prev()
            return (g, n) if n < STEPS and g.exists() else None

        def pair_of(step, graph, lag):
            at = tile_of(step, graph, lag)
            if at and at[1] % (2 * T) == T:
                return at[0], at[1] // (2 * T)
            return None

        def walk(eng, head, job):
            head(Graph(0))
            job(Graph(0), range(STEPS))
            job(Graph(1), range(STEPS))
            with eng.Fori(0, (B - 4) // 2) as i:
                job(Graph(2, i), range(STEPS))
                job(Graph(3, i), range(STEPS))
            job(Graph(B - 2), range(STEPS))
            job(Graph(B - 1), range(STEPS))
            job(Graph(B), range(tail))

        block = ctx.enter_context(nc.Block())

        @block.sync
        def _(sp):
            def load_adj(g):
                wait(sp, masked_done, g.prev().count(STEPS, 0))
                sp.dma_start(bias[:, g.slot()], adj[g.number()].rearrange("(t p) n -> p t n", p=P)
                             ).then_inc(adj_loaded[g.slot()], 16)

            def load_next(g, t):
                wait(sp, h_done, g.prev().count(T, t + 1))
                sp.dma_start(x_next[:, t], x_in[g.number(), t * P:(t + 1) * P, :]).then_inc(next_loaded[t], 16)

            def load_x(g):
                for t in range(T):
                    wait(sp, x_stored[t], g.count(16, 0))
                    sp.dma_start(x_sb[:, t], x_in[g.number(), t * P:(t + 1) * P, :]).then_inc(x_loaded[t], 16)

            def store_x(g):
                for t in range(T):
                    if first:
                        wait(sp, updated, g.count(PAIRS, PAIRS))
                    else:
                        wait(sp, taken["project"], g.count(T, t + 1))
                    sp.dma_start(x_out[g.number(), t * P:(t + 1) * P, :], x_sb[:, t]).then_inc(x_stored[t], 16)

            def stack(g, grp):
                slot = g.group_slot(grp)
                wait(sp, taken["qk"], g.count(2 * G, 2 * grp + 2))
                for j in range(GH):
                    for r, pick in enumerate((slice(0, 3, 2), slice(0, 4, 3), slice(1, 3))):
                        sp.dma_start(qk_stack[r * HD:(r + 1) * HD, slot, :, j, :].bitcast(F32),
                                     qk_parts[j * HD:(j + 1) * HD, pick, :].bitcast(F32)
                                     ).then_inc(stacked[slot][j], 16)

            for t in range(T):
                load_next(Graph(0), t)
            for n, name in enumerate(names):
                sp.dma_start(w_raw[name], w_in[name].rearrange("(c p) n -> p c n", p=P)).then_inc(w_loaded[name], 16)
                if n == 1:
                    sp.dma_start(row_bias[:], b_in["v" if first else "o"].partition_broadcast(P)
                                 ).then_inc(consts_in, 16)
                    if first:
                        sp.dma_start(qk_bias[:, 0, :], b_in["q"].rearrange("(g p) -> p g", p=P),
                                     allow_slow_non_contiguous=True).then_inc(consts_in, 16)
                        sp.dma_start(qk_bias[:, 1, :], b_in["k"].rearrange("(g p) -> p g", p=P),
                                     allow_slow_non_contiguous=True).then_inc(consts_in, 16)
                        sp.dma_start(beta_col[:], beta.partition_broadcast(P)).then_inc(consts_in, 16)
                    else:
                        sp.dma_start(row_raw[:], b_in["v"].unsqueeze(0)).then_inc(consts_in, 16)
            sp.dma_start(bias[:, 0], adj[0].rearrange("(t p) n -> p t n", p=P)).then_inc(adj_loaded[0], 16)

            def job(g, steps):
                if g.next().exists():
                    for t in range(T):
                        load_next(g.next(), t)
                done, due = (g.prev(), g) if first else (g.prev().prev(), g.prev())
                if not first:
                    if done.exists():
                        store_x(done)
                    if due.exists():
                        load_x(due)
                if g.next().exists():
                    load_adj(g.next())
                if g.exists():
                    stack(g, 1)
                if first and done.exists():
                    store_x(done)
                if g.exists():
                    if first:
                        load_x(g)
                    stack(g, 2)
                if g.next().exists():
                    stack(g.next(), 0)
                if not first and not g.exists():
                    store_x(g.prev())

            walk(sp, lambda g: stack(g, 0), job)
            for t in range(T):
                sp.wait_ge(x_stored[t], 16 * B)

        @block.gpsimd
        def _(pool):
            nc.gpsimd.memset(ident[:], 0.0)
            nc.gpsimd.memset(fold[:], 0.0)
            if not first:
                nc.gpsimd.memset(one_rows[:].bitcast(F32), 0.0)
                nc.gpsimd.memset(v_row[:].bitcast(F32), 0.0)
            nc.gpsimd.memset(eps[:], EPS)
            nc.gpsimd.memset(neg_half[:], -0.5)
            nc.gpsimd.memset(one_half[:], 1.5).then_inc(consts, 1)
            pool.wait_ge(consts, 1)
            if not first:
                nc.gpsimd.memset(one_rows[0:1, :].bitcast(F32), 1.0).then_inc(consts, 1)
                pool.wait_ge(consts, 2)
                nc.gpsimd.memset(one_rows[HD:HD + 1, :].bitcast(F32), 1.0).then_inc(consts, 1)
                pool.wait_ge(consts, 3)
            nc.gpsimd.affine_select(out=ident[:], in_=ident[:], compare_op=ALU.not_equal, fill=1.0, base=0,
                                    pattern=[[-1, P]], channel_multiplier=1).then_inc(consts, 1)
            for r in range(2):
                view = fold[:].rearrange("p (b c) -> p b c", b=2)
                nc.gpsimd.affine_select(out=view, in_=view, compare_op=ALU.not_equal, fill=1.0, base=-HD * r,
                                        pattern=[[-2 * HD, 2], [-1, HD]], channel_multiplier=1
                                        ).then_inc(consts, 1)
                pool.wait_ge(consts, CONSTS - 1 + r)

            def inverse_deviation(g):
                pool.wait_ge(mv_done, g.count(1, 1))
                wait(pool, h_done, g.count(T, 0))
                nc.gpsimd.tensor_tensor(var_eps[:], mean_var[:, :, 1], eps[:], ALU.add).then_inc(ln_steps, 1)
                pool.wait_ge(ln_steps, g.count(LN_STEPS, 1))
                nc.gpsimd.tensor_tensor(root0[:], var_eps[:], neg_half[:], ALU.pow).then_inc(ln_steps, 1)
                pool.wait_ge(ln_steps, g.count(LN_STEPS, 2))
                nc.gpsimd.tensor_tensor(sq[:], root0[:], root0[:], ALU.mult).then_inc(ln_steps, 1)
                nc.gpsimd.tensor_tensor(half_var[:], var_eps[:], neg_half[:], ALU.mult).then_inc(ln_steps, 1)
                nc.gpsimd.tensor_scalar(neg_mean[:], mean_var[:, :, 0], -1.0, None, ALU.mult).then_inc(ln_steps, 1)
                pool.wait_ge(ln_steps, g.count(LN_STEPS, 5))
                nc.gpsimd.tensor_tensor(prod[:], sq[:], half_var[:], ALU.mult).then_inc(ln_steps, 1)
                pool.wait_ge(ln_steps, g.count(LN_STEPS, 6))
                nc.gpsimd.tensor_tensor(fix[:], prod[:], one_half[:], ALU.add).then_inc(ln_steps, 1)
                pool.wait_ge(ln_steps, g.count(LN_STEPS, 7))
                nc.gpsimd.tensor_tensor(rstd[:], root0[:], fix[:], ALU.mult).then_inc(ln_steps, 1)
                pool.wait_ge(ln_steps, g.count(LN_STEPS, 8))
                nc.gpsimd.tensor_tensor(shift[:], neg_mean[:], rstd[:], ALU.mult).then_inc(ln_steps, 1)

            def make_bias(g, t):
                tile = bias[:, g.slot(), t, :]
                if t == 0:
                    pool.wait_ge(adj_loaded[g.slot()], g.slot_count(16))
                wait(pool, bias_done, g.count(T, t))
                nc.gpsimd.tensor_tensor(scaled[:], tile, beta_col[:].broadcast_to([P, N]), ALU.mult
                                        ).then_inc(bias_steps, 1)
                nc.gpsimd.tensor_scalar(hole[:], tile, 0.0, MASKED, ALU.is_le, ALU.mult).then_inc(bias_steps, 1)
                pool.wait_ge(bias_steps, g.count(2 * T, 2 * t + 2))
                nc.gpsimd.tensor_tensor(tile, scaled[:], hole[:], ALU.add).then_inc(bias_done, 1)

            def add_row_bias(g, t):
                pool.wait_ge(x_loaded[t], g.count(16, 16))
                if g.i is None and g.c == 0 and t == 0:
                    pool.wait_ge(consts_in, 16 * CONSTS_IN)
                nc.gpsimd.tensor_tensor(x_sb[:, t], x_sb[:, t], row_bias[:], ALU.add).then_inc(biased, 1)

            def update_x(g, p):
                pool.wait_ge(taken["turn_out"], g.count(PAIRS, p + 1))
                if p == 0:
                    pool.wait_ge(biased, g.count(T, T))
                cols = x_sb[:, :, p * 2 * HD:(p + 1) * 2 * HD]
                nc.gpsimd.tensor_tensor(cols, cols, update[:, p % 2], ALU.add).then_inc(updated, 1)

            def total_of(g, n):
                u, t = n // T, n % T
                pool.wait_ge(masked_done, g.count(STEPS, n + 1))
                if t == 0:
                    wait(pool, total_done, g.count(H, u - 1))
                nc.gpsimd.tensor_tensor(halves[:, u % 2, t, :], masked[:, n % 4, 0:N // 2],
                                        masked[:, n % 4, N // 2:N], ALU.add).then_inc(halved, 1)
                if t == T - 1:
                    pool.wait_ge(halved, g.count(STEPS, n + 1))
                    for level, w in enumerate((N // 4, N // 8, N // 16)):
                        nc.gpsimd.tensor_tensor(halves[:, u % 2, :, 0:w], halves[:, u % 2, :, 0:w],
                                                halves[:, u % 2, :, w:2 * w], ALU.add).then_inc(folded, 1)
                        pool.wait_ge(folded, g.count(3 * H, 3 * u + level + 1))

            def head(g):
                inverse_deviation(g)
                nc.gpsimd.memset(v_stack[:].bitcast(F32), 0.0).then_inc(consts, 1)
                if first:
                    pool.wait_ge(consts_in, 16 * CONSTS_IN)
                    for t in range(T):
                        make_bias(g, t)

            def job(g, steps):
                for step in steps:
                    if not first and g.exists():
                        total_of(g, step)
                    of = g if first else g.prev()
                    if of.exists() and step in ROW_BIAS_STEPS[layer]:
                        add_row_bias(of, ROW_BIAS_STEPS[layer].index(step))
                    if first and g.next().exists() and step in BIAS_STEPS:
                        make_bias(g.next(), BIAS_STEPS.index(step))
                    if step == moments_step + 1 and g.exists() and g.next().exists():
                        inverse_deviation(g.next())
                    at = pair_of(step, g, LAG_NORM)
                    if first and at:
                        update_x(*at)

            walk(pool, head, job)

        @block.scalar
        def _(act):
            def apply_norm(g, t):
                if t == 0:
                    act.wait_ge(ln_steps, g.count(LN_STEPS, LN_STEPS))
                wait(act, made["turn_h"], g.count(T, max(t - 1, 0)))
                nc.scalar.activation(h[:, t % 2, :], x_next[:, t, :], ACT.Relu, bias=shift[:, t:t + 1],
                                     scale=rstd[:, t:t + 1]).then_inc(h_done, 1)

            def upper_part(kind, k, g, bank):
                act.wait_ge(made[kind], g.count(per[kind], k + 1))
                if kind == "turn_h":
                    nc.scalar.activation(ht_hi[:, :, k * P:(k + 1) * P],
                                         m_ps[:, bank, 0:D].rearrange("p (c n) -> p c n", c=C),
                                         ACT.Copy).then_inc(upper[kind], 1)
                elif kind == "turn_a":
                    nc.scalar.activation(at_hi[:, k], m_ps[:, bank, 0:D].rearrange("p (c n) -> p c n", c=C),
                                         ACT.Copy).then_inc(upper[kind], 1)
                elif kind == "value":
                    if g.i is None and g.c == 0 and k == 0:
                        act.wait_ge(consts, CONSTS + 1)
                    nc.scalar.activation(v_stack[:, k, :, 0:3:2, 0:HD],
                                         m_ps[:, bank, 0:D].rearrange("p (a b d) -> p a b d", b=2, d=HD),
                                         ACT.Copy).then_inc(upper[kind], 1)
                elif kind == "qk":
                    grp, which = k // 2, k % 2
                    if which == 0 and not (g.i is None and g.c == 0 and grp == 0):
                        for j in range(GH):
                            act.wait_ge(stacked[1 - g.group_slot(grp)][j], g.group_count(grp, 16 * STACKS, 1))
                    if first:
                        nc.scalar.activation(qk_parts[:, 2 * which, :], m_ps[:, bank, :], ACT.Identity,
                                             bias=qk_bias[:, which, grp:grp + 1]).then_inc(upper[kind], 1)
                    else:
                        nc.scalar.activation(qk_parts[:, 2 * which, :], m_ps[:, bank, :],
                                             ACT.Copy).then_inc(upper[kind], 1)

            def split_weights(some):
                for name in some:
                    act.wait_ge(w_loaded[name], 16)
                    nc.scalar.activation(w_hi[name][:], w_raw[name], ACT.Copy, scale=scale[name]).then_inc(w_upper, 1)

            def head(g):
                split_weights(names[:2])
                apply_norm(g, 0)
                apply_norm(g, 1)
                for t in range(T):
                    upper_part("turn_h", t, g, bank_of("turn_h", t))
                    if t + 2 < T:
                        apply_norm(g, t + 2)
                for k in range(2):
                    upper_part("qk", k, g, bank_of("qk", k))
                split_weights(names[2:])
                if not first:
                    act.wait_ge(consts_in, 16 * CONSTS_IN)
                    act.wait_ge(consts, 1)
                    nc.scalar.activation(v_row[0:1, :], row_raw[:], ACT.Copy).then_inc(w_upper, 1)
                for k in range(2, ahead):
                    upper_part("qk", k, g, bank_of("qk", k))

            def job(g, steps):
                for step in steps:
                    at = pair_of(step, g, LAG_COPY)
                    if at:
                        act.wait_ge(weighed, at[0].count(STEPS, (2 * at[1] + 2) * T))
                        wait(act, made["turn_out"], at[0].count(PAIRS, at[1]))
                        nc.scalar.activation(out_t[:], o_ps[:], ACT.Copy).then_inc(out_copied, 1)
                    for kind, k, of, _ in tasks_at(step - 1, g, -1):
                        if kind in upper:
                            upper_part(kind, k, of, bank_of(kind, k))
                    for kind, k, of, _ in tasks_at(step + 2, g, 0):
                        if kind == "turn_h":
                            apply_norm(of, k)
                    at = tile_of(step, g, LAG_TURN)
                    if at:
                        of, n = at
                        u, t = n // T, n % T
                        act.wait_ge(turned, of.count(STEPS, n + 1))
                        if t == 0:
                            wait(act, weighed, of.count(STEPS, (u - 1) * T))
                        nc.scalar.activation(pt_hi[:, u % 2, :, t * P:(t + 1) * P],
                                             t_ps[:, n % 3, :].rearrange("p (c q) -> p c q", c=T),
                                             ACT.Copy).then_inc(hi_done, 1)
                    if g.exists():
                        n = step
                        u, t = n // T, n % T
                        act.wait_ge(masked_done, g.count(STEPS, n + 1))
                        wait(act, turned, g.count(STEPS, n - 3))
                        if n == 0 and g.prev().exists():
                            act.wait_ge(rsum_done, g.prev().count(PAIRS, 1))
                        nc.scalar.activation(probs[:, n % 4, :], masked[:, n % 4, :], ACT.Exp,
                                             bias=neg_max[:, g.slot(), u, t:t + 1], scale=-1.0,
                                             accum_out=sums[:, g.slot(), u, t:t + 1]).then_inc(probs_done, 1)

            walk(act, head, job)

        @block.vector
        def _(dve):
            def lower_part(kind, k, g, bank):
                if kind == "project":
                    dve.wait_ge(made[kind], g.count(T, k + 1))
                    dve.wait_ge(biased, g.count(T, k + 1))
                    row = x_sb[:, k, :]
                    nc.vector.tensor_tensor(row, m_ps[:, bank, 0:D], row, ALU.add).then_inc(taken[kind], 1)
                    return
                dve.wait_ge(upper[kind], g.count(per[kind], k + 1))
                if kind == "turn_h":
                    cols = slice(k * P, (k + 1) * P)
                    nc.vector.tensor_tensor(ht_lo[:, :, cols], m_ps[:, bank, 0:D].rearrange("p (c n) -> p c n", c=C),
                                            ht_hi[:, :, cols].bitcast(F32), ALU.subtract).then_inc(taken[kind], 1)
                elif kind == "turn_a":
                    nc.vector.tensor_tensor(at_lo[:, k], m_ps[:, bank, 0:D].rearrange("p (c n) -> p c n", c=C),
                                            at_hi[:, k].bitcast(F32), ALU.subtract).then_inc(taken[kind], 1)
                elif kind == "value":
                    nc.vector.tensor_tensor(v_stack[:, k, :, 0:3:2, HD:2 * HD],
                                            m_ps[:, bank, 0:D].rearrange("p (a b d) -> p a b d", b=2, d=HD),
                                            v_stack[:, k, :, 0:3:2, 0:HD].bitcast(F32), ALU.subtract
                                            ).then_inc(taken[kind], 1)
                elif kind == "qk":
                    grp, which = k // 2, k % 2
                    if first:
                        nc.vector.scalar_tensor_tensor(out=qk_parts[:, 2 * which + 1, :], in0=m_ps[:, bank, :],
                                                       scalar=qk_bias[:, which, grp:grp + 1],
                                                       in1=qk_parts[:, 2 * which, :].bitcast(F32), op0=ALU.add,
                                                       op1=ALU.subtract).then_inc(taken[kind], 1)
                    else:
                        nc.vector.tensor_tensor(qk_parts[:, 2 * which + 1, :], m_ps[:, bank, :],
                                                qk_parts[:, 2 * which, :].bitcast(F32), ALU.subtract
                                                ).then_inc(taken[kind], 1)

            def statistics(g, t):
                dve.wait_ge(next_loaded[t], g.count(16, 16))
                nc.vector.bn_stats(stat[:, t, :], x_next[:, t, :]).then_inc(stat_done, 1)

            def moments_wait(g):
                dve.wait_ge(stat_done, g.count(T, T))
                wait(dve, ln_steps, g.count(LN_STEPS, 0))

            def moments():
                for t in range(T):
                    last = nc.vector.bn_aggr(mean_var[:, t, :], stat[:, t, :])
                last.then_inc(mv_done, 1)

            def split_weights(some):
                for name in some:
                    dve.wait_ge(w_upper, names.index(name) + 1)
                    nc.vector.scalar_tensor_tensor(out=w_lo[name][:].rearrange("p c n -> p (c n)"),
                                                   in0=w_raw[name].rearrange("p c n -> p (c n)"), scalar=scale[name],
                                                   in1=w_hi[name][:].rearrange("p c n -> p (c n)").bitcast(F32),
                                                   op0=ALU.mult, op1=ALU.subtract).then_inc(w_split, 1)

            def head(g):
                for t in range(T):
                    statistics(g, t)
                moments_wait(g)
                moments()
                split_weights(names[:2])
                if first:
                    dve.wait_ge(consts_in, 16 * CONSTS_IN)
                    nc.vector.tensor_scalar(qk_bias[:, 0, :], qk_bias[:, 0, :], scale["q"], None, ALU.mult
                                            ).then_inc(w_split, 1)
                for t in range(T):
                    lower_part("turn_h", t, g, bank_of("turn_h", t))
                for k in range(2):
                    lower_part("qk", k, g, bank_of("qk", k))
                split_weights(names[2:])
                if not first:
                    dve.wait_ge(w_upper, len(names) + 1)
                    nc.vector.tensor_tensor(v_row[HD:HD + 1, :], row_raw[:], v_row[0:1, :].bitcast(F32),
                                            ALU.subtract).then_inc(w_split, 1)
                for k in range(2, ahead):
                    lower_part("qk", k, g, bank_of("qk", k))
                if first:
                    dve.wait_ge(bias_done, T)
                else:
                    dve.wait_ge(adj_loaded[0], 16)

            def out_rows(g, p, stage):
                sl = g.slot()
                mine = slice(2 * p, 2 * p + 2)
                if stage == 0:
                    dve.wait_ge(probs_done, g.count(STEPS, (2 * p + 2) * T))
                    wait(dve, taken["turn_out"], g.count(PAIRS, p - 1))
                    nc.vector.reciprocal(rsum[:, p % 2], sums[:, sl, mine, :]).then_inc(rsum_done, 1)
                    if not first:
                        dve.wait_ge(total_done, g.count(H, 2 * p + 2))
                        wait(dve, kept_done, g.count(PAIRS, p))
                        nc.vector.scalar_tensor_tensor(
                            out=size[:].rearrange("p h t -> p (h t)"),
                            in0=neg_max[:, sl, mine, :].rearrange("p h t -> p (h t)"), scalar=0.0,
                            in1=total[:, sl, mine, :].rearrange("p h t -> p (h t)"), op0=ALU.not_equal, op1=ALU.max
                        ).then_inc(size_done, 1)
                elif stage == 1 and not first:
                    dve.wait_ge(size_done, g.count(PAIRS, p + 1))
                    dve.wait_ge(rsum_done, g.count(PAIRS, p + 1))
                    nc.vector.scalar_tensor_tensor(
                        out=kept[:, p % 2].rearrange("p h t -> p (h t)"), in0=size[:].rearrange("p h t -> p (h t)"),
                        scalar=0.0, in1=rsum[:, p % 2].rearrange("p h t -> p (h t)"), op0=ALU.is_gt, op1=ALU.mult
                    ).then_inc(kept_done, 1)
                elif stage == 2:
                    dve.wait_ge(made["turn_out"], g.count(PAIRS, p + 1))
                    factor = rsum if first else kept
                    if first:
                        dve.wait_ge(rsum_done, g.count(PAIRS, p + 1))
                        wait(dve, updated, g.count(PAIRS, p - 1))
                        out = update[:, p % 2].rearrange("p t (h d) -> p t h d", h=2)
                    else:
                        dve.wait_ge(kept_done, g.count(PAIRS, p + 1))
                        if p == 0:
                            wait(dve, made["turn_a"], g.count(T, 0))
                        out = attn[:, :, p * 2 * HD:(p + 1) * 2 * HD].rearrange("p t (h d) -> p t h d", h=2)
                    by = factor[:, p % 2].rearrange("p h t -> p t h").unsqueeze(3).broadcast_to([P, T, 2, HD])
                    turned_out = m_ps[:, bank_of("turn_out", p), 0:N // 2].rearrange("p (t h d) -> p t h d", t=T, h=2)
                    nc.vector.tensor_tensor(out, turned_out, by, ALU.mult).then_inc(taken["turn_out"], 1)

            def job(g, steps):
                for step in steps:
                    for kind, k, of, _ in tasks_at(step - 2, g, -1):
                        if kind != "turn_out":
                            lower_part(kind, k, of, bank_of(kind, k))
                    if g.exists() and g.next().exists():
                        if step in stats_steps:
                            statistics(g.next(), stats_steps.index(step))
                        if step == moments_step:
                            moments_wait(g.next())
                    for stage, lag in enumerate((LAG_COPY, LAG_OUT, LAG_NORM)):
                        at = pair_of(step, g, lag)
                        if at:
                            out_rows(*at, stage)
                    if not first:
                        at = tile_of(step, g, LAG_TOTAL)
                        if at and at[1] % T == 0:
                            of, u = at[0], at[1] // T
                            dve.wait_ge(folded, of.count(3 * H, 3 * u + 3))
                            nc.vector.tensor_reduce(total[:, of.slot(), u, :], halves[:, u % 2, :, 0:N // 16], AX.X,
                                                    ALU.add).then_inc(total_done, 1)
                    if g.exists():
                        n = step
                        dve.wait_ge(scores_done, g.count(STEPS, n + 1))
                        if n == 0 and not (g.i is None and g.c == 0):
                            if first:
                                dve.wait_ge(bias_done, g.count(T, T))
                            else:
                                dve.wait_ge(adj_loaded[g.slot()], g.slot_count(16))
                        wait(dve, probs_done, g.count(STEPS, n - 3))
                        if not first:
                            wait(dve, halved, g.count(STEPS, n - 3))
                    at = tile_of(step, g, LAG_LO)
                    if at:
                        of, n = at
                        u, t = n // T, n % T
                        dve.wait_ge(hi_done, of.count(STEPS, n + 1))
                        dst = (slice(None), u % 2, slice(None), slice(t * P, (t + 1) * P))
                        nc.vector.tensor_tensor(pt_lo[dst], t_ps[:, n % 3, :].rearrange("p (c q) -> p c q", c=T),
                                                pt_hi[dst].bitcast(F32), ALU.subtract).then_inc(lo_done, 1)
                    if g.exists():
                        n = step
                        u, t = n // T, n % T
                        nc.vector.tensor_tensor_reduce(
                            out=masked[:, n % 4, :], in0=s_ps[:, n % 2, :], in1=bias[:, g.slot(), t, :], scale=negate,
                            scalar=BIG, op0=ALU.add, op1=ALU.min, accum_out=neg_max[:, g.slot(), u, t:t + 1]
                        ).then_inc(masked_done, 1)
                        if step == moments_step and g.next().exists():
                            moments()

            walk(dve, head, job)

        @block.tensor
        def _(pe):
            def three_passes(out, a_hi, a_lo, b_hi, b_lo, row, part, parts):
                terms = [(a[c], b[c]) for c in range(C) for a, b in ((a_hi, b_hi), (a_hi, b_lo), (a_lo, b_hi))]
                if row is not None:
                    terms.append((one_rows[:], row[:]))
                for n in range(len(terms) * part // parts, len(terms) * (part + 1) // parts):
                    last = nc.tensor.matmul(out, *terms[n], start=n == 0, stop=n == len(terms) - 1)
                return last

            def make(kind, k, g, part=0, parts=1):
                out = m_ps[:, bank_of(kind, k), :]
                if part == 0:
                    bank_free(pe, kind, k, g)
                if kind == "turn_h":
                    pe.wait_ge(h_done, g.count(T, k + 1))
                    for c in range(C):
                        last = nc.tensor.transpose(out[:, c * P:(c + 1) * P], h[:, k % 2, c * P:(c + 1) * P], ident[:])
                elif kind == "turn_a":
                    pe.wait_ge(taken["turn_out"], g.count(PAIRS, PAIRS))
                    for c in range(C):
                        last = nc.tensor.transpose(out[:, c * P:(c + 1) * P], attn[:, k, c * P:(c + 1) * P], ident[:])
                elif kind == "project":
                    if part == 0:
                        pe.wait_ge(taken["turn_a"], g.count(T, k + 1))
                    last = three_passes(out[:, 0:D], *([x[:, k, c, :] for c in range(C)] for x in (at_hi, at_lo)),
                                        *([w["o"][:, c, :] for c in range(C)] for w in (w_hi, w_lo)), None, part, parts)
                elif kind == "value":
                    pe.wait_ge(taken["turn_h"], g.count(T, T))
                    rows = slice(k * P, (k + 1) * P)
                    last = three_passes(out[:, 0:D], *([x[:, c, rows] for c in range(C)] for x in (ht_hi, ht_lo)),
                                        *([w["v"][:, c, :] for c in range(C)] for w in (w_hi, w_lo)), None if first else v_row, part,
                                        parts)
                elif kind == "qk":
                    if part == 0:
                        pe.wait_ge(taken["turn_h"], g.count(T, T))
                    name, cols = "qk"[k % 2], slice(k // 2 * P, (k // 2 + 1) * P)
                    last = three_passes(out, *([w[name][:, c, cols] for c in range(C)] for w in (w_hi, w_lo)),
                                        *([x[:, c, :] for c in range(C)] for x in (ht_hi, ht_lo)), None, part, parts)
                elif kind == "turn_out":
                    pe.wait_ge(out_copied, g.count(PAIRS, k + 1))
                    for t in range(T * part // parts, T * (part + 1) // parts):
                        last = nc.tensor.matmul(out[:, t * 2 * HD:(t + 1) * 2 * HD], out_t[:, t * P:(t + 1) * P],
                                                fold[:], start=True, stop=True)
                if part == parts - 1:
                    last.then_inc(made[kind], 1)

            def weigh(g, u, c):
                if c == 0:
                    pe.wait_ge(lo_done, g.count(STEPS, (u + 1) * T))
                    if u % 2 == 0:
                        wait(pe, out_copied, g.count(PAIRS, u // 2))
                if u == 0:
                    pe.wait_ge(taken["value"], g.count(T, c + 1))
                values = v_stack[:, c, u // 2].rearrange("p a b -> p (a b)")
                values = values[:, 0:P] if u % 2 == 0 else values[:, 2 * HD:2 * HD + P]
                nc.tensor.matmul(o_ps[:], values, pt_hi[:, u % 2, c, :], start=u % 2 == 0 and c == 0, stop=False)
                nc.tensor.matmul(o_ps[:], values, pt_lo[:, u % 2, c, :], start=False,
                                 stop=u % 2 == 1 and c == T - 1).then_inc(weighed, 1)

            pe.wait_ge(consts, CONSTS)

            def head(g):
                for t in range(T):
                    make("turn_h", t, g)
                pe.wait_ge(w_split, 3 if first else 2)
                for k in range(ahead):
                    make("qk", k, g)
                pe.wait_ge(w_split, len(names) + 1)

            def job(g, steps):
                for step in steps:
                    if g.exists():
                        n = step
                        u, t = n // T, n % T
                        grp, j = u // GH, u % GH
                        slot = g.group_slot(grp)
                        if t == 0:
                            pe.wait_ge(stacked[slot][j], g.group_count(grp, 16 * STACKS))
                        wait(pe, masked_done, g.count(STEPS, n - 1))
                        nc.tensor.matmul(s_ps[:, n % 2, :], qk_stack[:, slot, 0, j, t * P:(t + 1) * P],
                                         qk_stack[:, slot, 1, j, :], start=True, stop=True).then_inc(scores_done, 1)
                    for lag in range(LAG_WEIGH[0][-1], LAG_WEIGH[1][0] - 1, -1):
                        at = tile_of(step, g, lag)
                        if at and at[1] % T == 0:
                            u = at[1] // T
                            for c in range(T):
                                if LAG_WEIGH[u % 2][c] == lag:
                                    weigh(at[0], u, c)
                    at = tile_of(step, g, LAG_TURN)
                    if at:
                        of, n = at
                        pe.wait_ge(probs_done, of.count(STEPS, n + 1))
                        wait(pe, lo_done, of.count(STEPS, n - 2))
                        for c in range(T):
                            last = nc.tensor.transpose(t_ps[:, n % 3, c * P:(c + 1) * P],
                                                       probs[:, n % 4, c * P:(c + 1) * P], ident[:])
                        last.then_inc(turned, 1)
                    for kind, k, of, parts in tasks_at(step, g, None):
                        for part, at in enumerate(parts):
                            if at == step:
                                make(kind, k, of, part, len(parts))

            walk(pe, head, job)


def graph_attention_kernel(nc, x, adj, q0, bq0, k0, bk0, v0, bv0, beta, q1, k1, v1, bv1, o1, bo1, out):
    between = nc.dram_tensor("between_dram", (B, N, D), F32, kind="Internal").ap()
    layer_pass(nc, 0, x, adj, {"q": q0, "k": k0, "v": v0}, {"q": bq0, "k": bk0, "v": bv0}, beta, between)
    layer_pass(nc, 1, between, adj, {"q": q1, "k": k1, "v": v1, "o": o1}, {"v": bv1, "o": bo1}, None, out)


def kernel(**inputs):
    import numpy as _np
    import concourse.bacc as _bacc
    from concourse import mybir as _mybir
    from concourse.bass_utils import run_bass_kernel_spmd as _run

    nc = _bacc.Bacc("TRN2", target_bir_lowering=False, num_devices=1, dynamic_dma_scratch_size=1024)
    names = ["x", "adj", "L0_gnn_Wq", "L0_gnn_bq", "L0_gnn_Wk", "L0_gnn_bk", "L0_gnn_Wv", "L0_gnn_bv",
             "L0_gnn_beta", "L1_gnn_Wq", "L1_gnn_Wk", "L1_gnn_Wv", "L1_gnn_bv", "L1_gnn_Wo", "L1_gnn_bo"]
    transposed = {"L1_gnn_Wq", "L1_gnn_Wk", "L1_gnn_Wv", "L1_gnn_Wo"}
    arrays, args = {}, []
    for name in names:
        a = _np.asarray(inputs[name])
        a = a.T if name in transposed else a
        a = _np.ascontiguousarray(a.reshape(1) if a.ndim == 0 else a)
        arrays[f"in_{name}_dram"] = a
        args.append(nc.dram_tensor(f"in_{name}_dram", a.shape, _mybir.dt.from_np(a.dtype), kind="ExternalInput").ap())
    out = nc.dram_tensor("out_dram", (16, 512, 384), _mybir.dt.float32, kind="ExternalOutput").ap()
    graph_attention_kernel(nc, *args, out)
    r = _run(nc, [arrays], core_ids=[0])
    return r.results[0]["out_dram"]
```
